# Optimizing a Trainium2 kernel written in Bass

```python
import numpy as np
import jax
import jax.numpy as jnp

def _softmax(x, axis=-1):
    return jax.nn.softmax(x, axis=axis)

def _gelu(x):
    return jax.nn.gelu(x, approximate=True)

def _silu(x):
    return jax.nn.silu(x)

def _sigmoid(x):
    return jax.nn.sigmoid(x)

def _layernorm(x, axis=-1, eps=1e-05):
    m = jnp.mean(x, axis=axis, keepdims=True)
    v = jnp.var(x, axis=axis, keepdims=True)
    return (x - m) / jnp.sqrt(v + eps)

def _scatter_add(tgt, idx, src, axis=0):
    return tgt.at[idx].add(src)

def _segment_sum(src, seg, n):
    return jax.ops.segment_sum(src, seg, n)
kernel_name = 'mk_early_fusion_d1_tok_img1024_r4_8b0485'

def setup_inputs(seed: int=0):
    np.random.seed(seed)
    _w = jnp.asarray

    def _rec_inputs():
        import jax
        import jax.numpy as jnp
        _rk = jax.random.key(seed)
        x = -0.000125008 + 0.999885 * jax.random.normal(jax.random.fold_in(_rk, 1), (4, 512, 256, 4), jnp.float32)
        txt = -8.03667e-05 + 0.656214 * jax.random.normal(jax.random.fold_in(_rk, 2), (4, 512, 256), jnp.float32)
        return (x, txt)
    x, txt = _rec_inputs()

    def _L0_tok_setup():
        import jax, jax.numpy as jnp
        import numpy as np
        key = jax.random.key(seed)
        k1, k2, k3 = jax.random.split(key, 3)
        B, H, I, O, Dp1 = (4, 512, 256, 256, 4)
        x = jax.random.normal(k1, (B, H, I, Dp1), dtype=jnp.float32)
        weight = 0.1 * jax.random.normal(k2, (O, Dp1), dtype=jnp.float32)
        weighted_sum = 0.1 * jax.random.normal(k3, (O, I), dtype=jnp.float32)
        return {'x': x, 'weight': weight, 'weighted_sum': weighted_sum}
    _L0_tok_all = _L0_tok_setup()
    _L0_tok_in = {k: v for k, v in _L0_tok_all.items() if k in ('weight', 'weighted_sum')}
    del _L0_tok_all

    def _L0_attn_setup():
        import jax, jax.numpy as jnp
        import numpy as np
        DIM = 256
        HEADS = 16
        DIM_HEAD = 64
        SCALE = DIM_HEAD ** (-0.5)

        def _split_heads(t):
            b, n, _ = t.shape
            return t.reshape(b, n, HEADS, DIM_HEAD).transpose(0, 2, 1, 3)
        key = jax.random.key(seed)
        ks = jax.random.split(key, 7)
        init = lambda k, shape: jax.random.normal(k, shape, dtype=jnp.float32) * shape[0] ** (-0.5)
        return {'x': jax.random.normal(ks[0], (4, 1024, DIM), dtype=jnp.float32), 'Wq': init(ks[1], (DIM, HEADS * DIM_HEAD)), 'Wk': init(ks[2], (DIM, HEADS * DIM_HEAD)), 'Wv': init(ks[3], (DIM, HEADS * DIM_HEAD)), 'Wg': init(ks[4], (DIM, HEADS * DIM_HEAD)), 'bg': jnp.zeros((HEADS * DIM_HEAD,), dtype=jnp.float32), 'Wo': init(ks[5], (HEADS * DIM_HEAD, DIM))}
    _L0_attn_all = _L0_attn_setup()
    _L0_attn_in = {k: v for k, v in _L0_attn_all.items() if k in ('Wq', 'Wk', 'Wv', 'Wg', 'bg', 'Wo')}
    del _L0_attn_all

    def _L0_ffn_setup():
        import jax, jax.numpy as jnp
        import numpy as np
        DIM = 256
        DEPTH = 2
        HEADS = 8
        DIM_HEAD = 64
        WINDOW = 128
        INNER = HEADS * DIM_HEAD
        HID = int(DIM * 4 * 2 / 3)
        B, N = (2, 2048)
        QK_SCALE = 8.0

        def shift_token(t):
            t1, t2 = jnp.split(t, 2, axis=-1)
            t2 = jnp.pad(t2, ((0, 0), (1, 0), (0, 0)))[:, :-1]
            return jnp.concatenate([t1, t2], axis=-1)

        def l2norm(t):
            return t / jnp.clip(jnp.linalg.norm(t, axis=-1, keepdims=True), 1e-12)

        def rotate_half(x):
            x1, x2 = jnp.split(x, 2, axis=-1)
            return jnp.concatenate([-x2, x1], axis=-1)

        def rotary_xpos(q, k):
            n = q.shape[-2]
            half_idx = jnp.arange(0, DIM_HEAD, 2, dtype=jnp.float32)
            inv_freq = 1.0 / 10000.0 ** (half_idx / DIM_HEAD)
            t = jnp.arange(n, dtype=jnp.float32)
            freqs = t[:, None] * inv_freq[None, :]
            freqs = jnp.concatenate([freqs, freqs], axis=-1)
            base = (half_idx + 0.4 * DIM_HEAD) / (1.4 * DIM_HEAD)
            power = (t - n // 2) / float(WINDOW // 2)
            scale = base[None, :] ** power[:, None]
            scale = jnp.concatenate([scale, scale], axis=-1)
            cos, sin = (jnp.cos(freqs), jnp.sin(freqs))
            q = q * cos * scale + rotate_half(q) * sin * scale
            k = k * cos / scale + rotate_half(k) * sin / scale
            return (q, k)

        def local_attention(q, k, v):
            b, h, n, d = q.shape
            w = n // WINDOW
            bq = q.reshape(b, h, w, WINDOW, d) * QK_SCALE
            bk = k.reshape(b, h, w, WINDOW, d)
            bv = v.reshape(b, h, w, WINDOW, d)

            def look_around(t):
                p = jnp.pad(t, ((0, 0), (0, 0), (1, 0), (0, 0), (0, 0)))
                return jnp.concatenate([p[:, :, :w], p[:, :, 1:]], axis=3)
            bk, bv = (look_around(bk), look_around(bv))
            bt = jnp.arange(n).reshape(w, WINDOW)
            btp = jnp.pad(bt, ((1, 0), (0, 0)), constant_values=-1)
            btk = jnp.concatenate([btp[:w], btp[1:]], axis=1)
            sim = jnp.einsum('bhwid,bhwjd->bhwij', bq, bk)
            i = bt[:, :, None]
            j = btk[:, None, :]
            mask = (i < j) | (i > j + WINDOW) | (j == -1)
            sim = jnp.where(mask, -jnp.finfo(sim.dtype).max, sim)
            attn = jax.nn.softmax(sim, axis=-1)
            out = jnp.einsum('bhwij,bhwjd->bhwid', attn, bv)
            return out.reshape(b, h, n, d)

        def _layer(x, wqkv, qs, ksc, wo, lg, lb, w1, b1, w2, b2):
            b, n, _ = x.shape
            h = shift_token(x)
            qkv = h @ wqkv
            q, k, v = jnp.split(qkv, 3, axis=-1)
            to_heads = lambda t: t.reshape(b, n, HEADS, DIM_HEAD).transpose(0, 2, 1, 3)
            q, k, v = (to_heads(q), to_heads(k), to_heads(v))
            q = l2norm(q) * qs
            k = l2norm(k) * ksc
            q, k = rotary_xpos(q, k)
            o = local_attention(q, k, v)
            o = o.transpose(0, 2, 1, 3).reshape(b, n, INNER)
            x = x + o @ wo
            h = shift_token(x)
            mu = h.mean(-1, keepdims=True)
            var = h.var(-1, keepdims=True)
            h = (h - mu) / jnp.sqrt(var + 1e-05) * lg + lb
            h = h @ w1 + b1
            a, g = jnp.split(h, 2, axis=-1)
            h = a * jax.nn.gelu(g, approximate=False)
            x = x + h @ w2 + b2
            return x
        key = jax.random.key(seed)
        ks = jax.random.split(key, 6)
        return {'x': jax.random.normal(ks[0], (B, N, DIM), jnp.float32), 'wqkv': jax.random.normal(ks[1], (DEPTH, DIM, 3 * INNER), jnp.float32) * 0.02, 'q_scale': jnp.ones((DEPTH, DIM_HEAD), jnp.float32), 'k_scale': jnp.ones((DEPTH, DIM_HEAD), jnp.float32), 'wo': jax.random.normal(ks[2], (DEPTH, INNER, DIM), jnp.float32) * 0.02, 'ln_g': jnp.ones((DEPTH, DIM), jnp.float32), 'ln_b': jnp.zeros((DEPTH, DIM), jnp.float32), 'w1': jax.random.normal(ks[3], (DEPTH, DIM, 2 * HID), jnp.float32) * 0.02, 'b1': jnp.zeros((DEPTH, 2 * HID), jnp.float32), 'w2': jax.random.normal(ks[4], (DEPTH, HID, DIM), jnp.float32) * 0.02, 'b2': jnp.zeros((DEPTH, DIM), jnp.float32)}
    _L0_ffn_all = _L0_ffn_setup()
    _L0_ffn_in = {k: v for k, v in _L0_ffn_all.items() if k in ('wqkv', 'q_scale', 'k_scale', 'wo', 'ln_g', 'ln_b', 'w1', 'b1', 'w2', 'b2')}
    del _L0_ffn_all
    return {'x': x, 'txt': txt, 'L0_tok_weight': _L0_tok_in['weight'], 'L0_tok_weighted_sum': _L0_tok_in['weighted_sum'], 'L0_attn_Wq': _L0_attn_in['Wq'], 'L0_attn_Wk': _L0_attn_in['Wk'], 'L0_attn_Wv': _L0_attn_in['Wv'], 'L0_attn_Wg': _L0_attn_in['Wg'], 'L0_attn_bg': _L0_attn_in['bg'], 'L0_attn_Wo': _L0_attn_in['Wo'], 'L0_ffn_wqkv': _L0_ffn_in['wqkv'], 'L0_ffn_q_scale': _L0_ffn_in['q_scale'], 'L0_ffn_k_scale': _L0_ffn_in['k_scale'], 'L0_ffn_wo': _L0_ffn_in['wo'], 'L0_ffn_ln_g': _L0_ffn_in['ln_g'], 'L0_ffn_ln_b': _L0_ffn_in['ln_b'], 'L0_ffn_w1': _L0_ffn_in['w1'], 'L0_ffn_b1': _L0_ffn_in['b1'], 'L0_ffn_w2': _L0_ffn_in['w2'], 'L0_ffn_b2': _L0_ffn_in['b2']}

def reference(x, txt, L0_tok_weight, L0_tok_weighted_sum, L0_attn_Wq, L0_attn_Wk, L0_attn_Wv, L0_attn_Wg, L0_attn_bg, L0_attn_Wo, L0_ffn_wqkv, L0_ffn_q_scale, L0_ffn_k_scale, L0_ffn_wo, L0_ffn_ln_g, L0_ffn_ln_b, L0_ffn_w1, L0_ffn_b1, L0_ffn_w2, L0_ffn_b2):
    import jax
    import jax.numpy as jnp

    def _L0_tok_ref(x, weight, weighted_sum):
        import jax, jax.numpy as jnp
        import numpy as np
        return jnp.einsum('bhid,oi,od->bho', x, weighted_sum, weight)

    def _L0_attn_ref(x, Wq, Wk, Wv, Wg, bg, Wo):
        import jax, jax.numpy as jnp
        import numpy as np
        DIM = 256
        HEADS = 16
        DIM_HEAD = 64
        SCALE = DIM_HEAD ** (-0.5)

        def _split_heads(t):
            b, n, _ = t.shape
            return t.reshape(b, n, HEADS, DIM_HEAD).transpose(0, 2, 1, 3)
        q = _split_heads(x @ Wq)
        k = _split_heads(x @ Wk)
        v = _split_heads(x @ Wv)
        g = _split_heads(x @ Wg + bg)
        q = jax.nn.elu(q) + 1.0
        k = jax.nn.elu(k) + 1.0
        g = jax.nn.sigmoid(g)
        kv = jnp.einsum('bhnd,bhne->bhde', k, v)
        k_sum = k.sum(axis=-2)
        z = 1.0 / jnp.clip(jnp.einsum('bhnd,bhd->bhn', q, k_sum), 1e-06)
        out = jnp.einsum('bhnd,bhde->bhne', q * SCALE, kv)
        out = out * z[..., None] * g
        b, h, n, d = out.shape
        out = out.transpose(0, 2, 1, 3).reshape(b, n, h * d)
        return out @ Wo

    def _L0_ffn_ref(x, wqkv, q_scale, k_scale, wo, ln_g, ln_b, w1, b1, w2, b2):
        import jax, jax.numpy as jnp
        import numpy as np
        DIM = 256
        DEPTH = 2
        HEADS = 8
        DIM_HEAD = 64
        WINDOW = 128
        INNER = HEADS * DIM_HEAD
        HID = int(DIM * 4 * 2 / 3)
        B, N = (2, 2048)
        QK_SCALE = 8.0

        def shift_token(t):
            t1, t2 = jnp.split(t, 2, axis=-1)
            t2 = jnp.pad(t2, ((0, 0), (1, 0), (0, 0)))[:, :-1]
            return jnp.concatenate([t1, t2], axis=-1)

        def l2norm(t):
            return t / jnp.clip(jnp.linalg.norm(t, axis=-1, keepdims=True), 1e-12)

        def rotate_half(x):
            x1, x2 = jnp.split(x, 2, axis=-1)
            return jnp.concatenate([-x2, x1], axis=-1)

        def rotary_xpos(q, k):
            n = q.shape[-2]
            half_idx = jnp.arange(0, DIM_HEAD, 2, dtype=jnp.float32)
            inv_freq = 1.0 / 10000.0 ** (half_idx / DIM_HEAD)
            t = jnp.arange(n, dtype=jnp.float32)
            freqs = t[:, None] * inv_freq[None, :]
            freqs = jnp.concatenate([freqs, freqs], axis=-1)
            base = (half_idx + 0.4 * DIM_HEAD) / (1.4 * DIM_HEAD)
            power = (t - n // 2) / float(WINDOW // 2)
            scale = base[None, :] ** power[:, None]
            scale = jnp.concatenate([scale, scale], axis=-1)
            cos, sin = (jnp.cos(freqs), jnp.sin(freqs))
            q = q * cos * scale + rotate_half(q) * sin * scale
            k = k * cos / scale + rotate_half(k) * sin / scale
            return (q, k)

        def local_attention(q, k, v):
            b, h, n, d = q.shape
            w = n // WINDOW
            bq = q.reshape(b, h, w, WINDOW, d) * QK_SCALE
            bk = k.reshape(b, h, w, WINDOW, d)
            bv = v.reshape(b, h, w, WINDOW, d)

            def look_around(t):
                p = jnp.pad(t, ((0, 0), (0, 0), (1, 0), (0, 0), (0, 0)))
                return jnp.concatenate([p[:, :, :w], p[:, :, 1:]], axis=3)
            bk, bv = (look_around(bk), look_around(bv))
            bt = jnp.arange(n).reshape(w, WINDOW)
            btp = jnp.pad(bt, ((1, 0), (0, 0)), constant_values=-1)
            btk = jnp.concatenate([btp[:w], btp[1:]], axis=1)
            sim = jnp.einsum('bhwid,bhwjd->bhwij', bq, bk)
            i = bt[:, :, None]
            j = btk[:, None, :]
            mask = (i < j) | (i > j + WINDOW) | (j == -1)
            sim = jnp.where(mask, -jnp.finfo(sim.dtype).max, sim)
            attn = jax.nn.softmax(sim, axis=-1)
            out = jnp.einsum('bhwij,bhwjd->bhwid', attn, bv)
            return out.reshape(b, h, n, d)

        def _layer(x, wqkv, qs, ksc, wo, lg, lb, w1, b1, w2, b2):
            b, n, _ = x.shape
            h = shift_token(x)
            qkv = h @ wqkv
            q, k, v = jnp.split(qkv, 3, axis=-1)
            to_heads = lambda t: t.reshape(b, n, HEADS, DIM_HEAD).transpose(0, 2, 1, 3)
            q, k, v = (to_heads(q), to_heads(k), to_heads(v))
            q = l2norm(q) * qs
            k = l2norm(k) * ksc
            q, k = rotary_xpos(q, k)
            o = local_attention(q, k, v)
            o = o.transpose(0, 2, 1, 3).reshape(b, n, INNER)
            x = x + o @ wo
            h = shift_token(x)
            mu = h.mean(-1, keepdims=True)
            var = h.var(-1, keepdims=True)
            h = (h - mu) / jnp.sqrt(var + 1e-05) * lg + lb
            h = h @ w1 + b1
            a, g = jnp.split(h, 2, axis=-1)
            h = a * jax.nn.gelu(g, approximate=False)
            x = x + h @ w2 + b2
            return x
        for l in range(DEPTH):
            x = _layer(x, wqkv[l], q_scale[l], k_scale[l], wo[l], ln_g[l], ln_b[l], w1[l], b1[l], w2[l], b2[l])
        return x
    h = _L0_tok_ref(x, L0_tok_weight, L0_tok_weighted_sum)
    h = jnp.concatenate([h, txt], axis=1)
    h = h + _L0_attn_ref(_layernorm(h, axis=-1), L0_attn_Wq, L0_attn_Wk, L0_attn_Wv, L0_attn_Wg, L0_attn_bg, L0_attn_Wo)
    h = h + _L0_ffn_ref(_layernorm(h, axis=-1), L0_ffn_wqkv, L0_ffn_q_scale, L0_ffn_k_scale, L0_ffn_wo, L0_ffn_ln_g, L0_ffn_ln_b, L0_ffn_w1, L0_ffn_b1, L0_ffn_w2, L0_ffn_b2)
    return h

_drawn_inputs = setup_inputs


def setup_inputs(seed=0):
    import zlib

    import numpy as np

    out = dict(_drawn_inputs(seed))
    spreads = {'L0_attn_bg': (0.0, 0.8),
     'L0_ffn_q_scale': (1.0, 0.6),
     'L0_ffn_k_scale': (1.0, 0.6),
     'L0_ffn_ln_g': (1.0, 0.6),
     'L0_ffn_ln_b': (0.0, 0.8),
     'L0_ffn_b1': (0.0, 0.609),
     'L0_ffn_b2': (0.0, 0.1)}
    factors = {'L0_attn_Wq': 8.0,
     'L0_attn_Wk': 8.0,
     'L0_attn_Wv': 8.0,
     'L0_attn_Wg': 8.0,
     'L0_attn_Wo': 8.0}
    for name, (base, spread) in spreads.items():
        noise = np.random.default_rng([zlib.crc32(name.encode()), seed]).standard_normal(out[name].shape)
        drawn = base * np.exp(spread * noise) if base else spread * noise
        out[name] = jnp.asarray(drawn.astype(out[name].dtype))
    for name, factor in factors.items():
        out[name] = (out[name] * factor).astype(out[name].dtype)
    return out
```

```python
import concourse.bass as bass
from concourse import mybir
from contextlib import ExitStack

F32 = mybir.dt.float32
F32R = mybir.dt.float32r
BF16 = mybir.dt.bfloat16
I32 = mybir.dt.int32
ALU = mybir.AluOpType
ACT = mybir.ActivationFunctionType
AX = mybir.AxisListType

P = 128
B, N, D = 4, 1024, 256
NIMG = 512
DP = 4
TB = N // P
T = B * TB
KC = D // P
HEADS, DH = 16, 64
INNER = HEADS * DH
PAIRS = HEADS // 2
LH = 8
LINNER = LH * DH
LPAIRS = LH // 2
HID = 682
HC = HID // P
HR = HID - HC * P
GR = 64
W1C = 2 * HC * P + GR + HR
LN_EPS = 1e-5
MASKED = -1.0e37
LOWEST = -3.0e38
RSQRT_SEED = float(0x5F3759DF)
ROPE_BASE = 10000.0
WINDOW = 128


class Memory:

    def __init__(self, nc):
        self.nc = nc
        base = (nc.sbuf_base + 63) // 64 * 64
        self.h = base
        self.x = self.h + T * D * 4
        self.const = self.x + T * D * 4
        self.wb = self.const + 5312
        self.wa = self.wb + 32768
        self.tail = self.wa + 81920
        self.end = nc.sbuf_usable_end

    def place(self, at, end, *wanted):
        out = []
        for name, shape, dt in wanted:
            size = 2 if dt == BF16 else 4
            for n in shape[1:]:
                size *= n
            out.append(self.nc.alloc_sbuf_tensor_at(name, shape, dt, offset=at))
            at += (size + 31) // 32 * 32
            assert at <= end, (name, at, end)
        return out, at


def f32(ap):
    return ap.bitcast(F32)


class Count:

    def __init__(self, sem, credit):
        self.sem, self.credit = sem, credit

    def after(self, n):
        return self.sem, self.credit + n

    def room(self, n, slots):
        return self.sem, self.credit + n + 1 - slots


class Chain:

    def __init__(self, eng, sem):
        self.eng, self.sem, self.base, self.n = eng, sem, 0, 0

    def __call__(self, ins):
        self.n += 1
        ins.then_inc(self.sem, 1)
        self.eng.wait_ge(self.sem, self.base + self.n)

    def rebase(self, base):
        self.base, self.n = base, 0


def matmul3(nc, out, wh, wl, mh, ml, start, stop):
    nc.tensor.matmul(out, wh, mh, start=start, stop=False, skip_group_check=True)
    nc.tensor.matmul(out, wh, ml, start=False, stop=False, skip_group_check=True)
    return nc.tensor.matmul(out, wl, mh, start=False, stop=stop, skip_group_check=True)


def rsqrt(nc, chain, out, tmp, val, steps=3):
    chain(nc.vector.tensor_scalar(out.bitcast(I32), val.bitcast(I32), -0.5, RSQRT_SEED, ALU.mult, ALU.add))
    for _ in range(steps):
        chain(nc.vector.tensor_tensor(tmp, out, out, ALU.mult))
        chain(nc.vector.scalar_tensor_tensor(tmp, tmp, -0.5, val, ALU.mult, ALU.mult))
        chain(nc.vector.scalar_tensor_tensor(out, tmp, 1.5, out, ALU.add, ALU.mult))



class Stats:

    def __init__(self, st, n, groups, mean, rstd, tmp, dev):
        self.st, self.n, self.groups, self.mean, self.rstd, self.tmp, self.dev = st, n, groups, mean, rstd, tmp, dev

    def finish(self, nc, chain):
        n, g = self.n, self.groups
        v = self.st.rearrange("p n (g k) -> p n g k", k=3)
        mean, rstd, tmp, dev = self.mean, self.rstd, self.tmp, self.dev
        chain(nc.vector.tensor_reduce(rstd, v[:, :, :, 1], AX.X, ALU.add))
        chain(nc.vector.tensor_scalar(mean, rstd, 1.0 / g, None, ALU.mult))
        chain(nc.vector.tensor_tensor(dev, v[:, :, :, 1], mean.unsqueeze(2).to_broadcast([P, n, g]), ALU.subtract))
        chain(nc.vector.tensor_tensor(dev, dev, dev, ALU.mult))
        chain(nc.vector.tensor_reduce(tmp, dev, AX.X, ALU.add))
        chain(nc.vector.tensor_reduce(rstd, v[:, :, :, 2], AX.X, ALU.add))
        chain(nc.vector.tensor_scalar(rstd, rstd, 1.0 / D, LN_EPS, ALU.mult, ALU.add))
        chain(nc.vector.scalar_tensor_tensor(dev[:, :, 0], tmp, 1.0 / g, rstd, ALU.mult, ALU.add))
        rsqrt(nc, chain, rstd, tmp, dev[:, :, 0])


STATS_STEPS = 8 + 10


def tok_phase(nc, s, mem, K, A):
    ps = K.ps
    NC = DP * KC
    JT = NIMG // P
    (xin, xth, xtl), _ = mem.place(mem.x, mem.const,
                                   ("tok_x", [P, JT, D * DP], F32),
                                   ("tok_xT_hi", [P, 2, NC, P], F32R),
                                   ("tok_xT_lo", [P, 2, NC, P], F32R))
    (wh, wl, ws, wrow), _ = mem.place(mem.tail, mem.end,
                                      ("tok_w_hi", [P, NC, D], F32R), ("tok_w_lo", [P, NC, D], F32R),
                                      ("tok_ws", [P, KC, D], F32), ("tok_wrow", [P, D * DP], F32))
    (wraw, bgrest, bgpart), _ = mem.place(mem.wb, mem.wa, ("tok_w_raw", [P, NC, D], F32),
                                          ("tok_bias_rest", [3, INNER], F32), ("tok_bias_part", [3, INNER], BF16))
    assert B == 4 and JT >= KC, "one of the four weight matrices of the attention is split a batch"
    x_t = A.x.rearrange("b (j p) i d -> b j p (i d)", p=P)
    with nc.Block() as block:

        @block.sync
        def _(sp):
            sp.dma_start(K.ident[:], A.ident).then_inc(s.ident.sem, 16)
            sp.dma_start(ws[:], A.tok_ws.rearrange("(c p) i -> p c i", p=P)).then_inc(s.tok_ws.sem, 16)
            sp.dma_start(wrow[:], A.tok_w.rearrange("(a o) d -> a (o d)", a=1).to_broadcast([P, D * DP])
                         ).then_inc(s.tok_wrow.sem, 16)
            with sp.Fori(0, B) as b:
                for j in range(JT):
                    sp.wait_ge(*s.tok_xt.room(2 * (JT * b + j) + 1, 2 * JT))
                    sp.dma_start(xin[:, j:j + 1, :], x_t[bass.ds(b, 1), j].rearrange("b p c -> p b c")
                                 ).then_inc(s.tok_in[j].sem, 16)
                sp.dma_start(K.H[:, bass.ds(TB * b + JT, TB - JT), :], A.txt.rearrange("b (j p) c -> p (b j) c", p=P)
                             [:, bass.ds((TB - JT) * b, TB - JT), :]).then_inc(s.txt_in.sem, 16)
            sp.wait_ge(*s.txt_in.after(16 * B))

        @block.scalar
        def _(act):
            act.dma_start(bgrest[:], K.attn_bias).then_inc(s.bias_in.sem, 16)
            for raw, src in K.attn_raw:
                act.dma_start(raw, src).then_inc(s.attn_w.sem, 16)
            for d in range(DP):
                act.wait_ge(*s.tok_wraw.after(d + 1))
                w = slice(d * KC, (d + 1) * KC)
                nc.scalar.activation(wh[:, w], wraw[:, w], ACT.Copy).then_inc(s.tok_whi.sem, 1)

            def take(b, j):
                act.wait_ge(*s.tok_mm.after(JT * b + j + 1))
                nc.scalar.activation(K.H[:, bass.ds(TB * b + j, 1), :], ps[:, 4 + j % 2:5 + j % 2, 0:D],
                                     ACT.Copy).then_inc(s.tok_h.sem, 1)

            with act.Fori(0, B) as b:
                for j in range(JT):
                    act.wait_ge(*s.tok_mm.room(JT * b + j, 2))
                    for half in range(2):
                        act.wait_ge(*s.tok_xt.after(2 * (JT * b + j) + half + 1))
                        nc.scalar.activation(xth[:, j % 2, 4 * half:4 * half + 4, :].rearrange("p c t -> p (c t)"),
                                             ps[:, 2 * (j % 2) + half, :], ACT.Copy).then_inc(s.tok_hi.sem, 1)
                    if j:
                        take(b, j - 1)
                    if j >= JT - KC:
                        c = j - (JT - KC)
                        act.wait_ge(*s.attn_w.after(16 * len(K.attn_raw)))
                        nc.scalar.activation(K.attn_wh[:, bass.ds(b, 1), c], K.attn_wraw[:, bass.ds(b, 1), c],
                                             ACT.Copy).then_inc(s.attn_whi.sem, 1)
                take(b, JT - 1)

        @block.vector
        def _(dve):
            chain = Chain(dve, s.bias.sem)
            rest, part, rows = bgrest, bgpart, K.attn_bgrows
            dve.wait_ge(*s.bias_in.after(16))
            dve.wait_ge(*s.ident.after(16))

            def bias_row(k):
                chain(nc.vector.tensor_copy(part[:], rest[:]))
                if k == 0:
                    chain(nc.vector.tensor_scalar(rows[:], part[:], K.ident[0:3, 0:1], None, ALU.mult))
                else:
                    chain(nc.vector.scalar_tensor_tensor(rows[:], part[:], K.ident[0:3, k:k + 1], rows[:],
                                                         ALU.mult, ALU.add))
                if k < 2:
                    chain(nc.vector.tensor_tensor(rest[:], rest[:], part[:], ALU.subtract))

            bias_row(0)
            bias_row(1)
            dve.wait_ge(*s.tok_wrow.after(16))
            dve.wait_ge(*s.tok_wst.after(1))
            wr = wrow[:].rearrange("p (o d) -> p o d", d=DP)
            for d in range(DP):
                for c in range(KC):
                    last = nc.vector.tensor_tensor(wraw[:, d * KC + c, :], ps[:, 6, c * D:(c + 1) * D],
                                                   wr[:, :, d], ALU.mult)
                last.then_inc(s.tok_wraw.sem, 1)
            bias_row(2)
            for d in range(DP):
                dve.wait_ge(*s.tok_whi.after(d + 1))
                w = slice(d * KC, (d + 1) * KC)
                nc.vector.tensor_tensor(wl[:, w], wraw[:, w], f32(wh[:, w]), ALU.subtract).then_inc(s.tok_wlo.sem, 1)
            with dve.Fori(0, B) as b:
                for j in range(JT):
                    for half in range(2):
                        dve.wait_ge(*s.tok_hi.after(2 * (JT * b + j) + half + 1))
                        nc.vector.tensor_tensor(
                            xtl[:, j % 2, 4 * half:4 * half + 4, :].rearrange("p c t -> p (c t)"),
                            ps[:, 2 * (j % 2) + half, :],
                            f32(xth[:, j % 2, 4 * half:4 * half + 4, :].rearrange("p c t -> p (c t)")),
                            ALU.subtract).then_inc(s.tok_lo.sem, 1)
                    if j >= JT - KC:
                        c = j - (JT - KC)
                        dve.wait_ge(*s.attn_whi.after(KC * b + c + 1))
                        w = bass.ds(b, 1)
                        nc.vector.tensor_tensor(K.attn_wl[:, w, c], K.attn_wraw[:, w, c], f32(K.attn_wh[:, w, c]),
                                                ALU.subtract)

        @block.tensor
        def _(pe):
            pe.wait_ge(*s.ident.after(16))
            pe.wait_ge(*s.tok_ws.after(16))
            for c in range(KC):
                for o in range(KC):
                    last = nc.tensor.transpose(ps[:, 6, c * D + o * P:c * D + (o + 1) * P],
                                               ws[:, o, c * P:(c + 1) * P], K.ident[:])
            last.then_inc(s.tok_wst.sem, 1)

            def transposes(b, j):
                pe.wait_ge(*s.tok_in[j].after(16 * b + 16))
                xv = xin[:, j, :].rearrange("p (c i d) -> p d c i", c=KC, d=DP)
                for half in range(2):
                    pe.wait_ge(*s.tok_lo.room(2 * (JT * b + j) + half, 4))
                    for k in range(4):
                        d, c = (4 * half + k) // KC, k % KC
                        last = nc.tensor.transpose(ps[:, 2 * (j % 2) + half, k * P:(k + 1) * P],
                                                   xv[:, d, c, :], K.ident[:])
                    last.then_inc(s.tok_xt.sem, 1)

            def products(b, j):
                pe.wait_ge(*s.tok_wlo.after(DP))
                pe.wait_ge(*s.tok_lo.after(2 * (JT * b + j) + 2))
                pe.wait_ge(*s.tok_h.room(JT * b + j, 2))
                for k in range(NC):
                    last = matmul3(nc, ps[:, 4 + j % 2, 0:D], xth[:, j % 2, k, :], xtl[:, j % 2, k, :],
                                   wh[:, k, :], wl[:, k, :], k == 0, k == NC - 1)
                last.then_inc(s.tok_mm.sem, 1)

            with pe.Fori(0, B) as b:
                for j in range(JT):
                    transposes(b, j)
                    if j:
                        products(b, j - 1)
                products(b, JT - 1)



def attention_phase(nc, s, mem, K, A):
    ps = K.ps
    H = K.H
    wh, wl = K.attn_wh, K.attn_wl
    woh, wol, woraw = K.attn_woh, K.attn_wol, K.attn_woraw
    Q, KEY, VAL, GATE = range(4)
    VC = P + 1
    OC = P + 2
    GROUPS = ((0, 3), (3, 6), (6, 8))
    HALF = INNER // 2
    (xth, xtl, th, og), _ = mem.place(
        mem.x, mem.const, ("attn_xT_hi", [P, KC, N], F32R), ("attn_xT_lo", [P, KC, N], F32R),
        ("attn_tanh", [P, 2, INNER], F32), ("attn_out", [P, 2, INNER], F32))
    (ks, vs, kv, oth, otl), _ = mem.place(
        mem.wb, mem.wa, ("attn_k", [P, 2, INNER], F32), ("attn_v", [P, 2, PAIRS, VC], F32),
        ("attn_kv", [P, PAIRS, OC], F32), ("attn_oT_hi", [P, PAIRS, P], F32R),
        ("attn_oT_lo", [P, PAIRS, P], F32R))
    (qt, ex, xn, o1, ones, mean, rs, tmp, dev, st, z, zd), _ = mem.place(
        mem.tail, mem.end, ("attn_qT", [P, PAIRS, 2 * P], F32), ("attn_exp", [P, 2, 512], F32),
        ("attn_xn", [P, 2, D], F32), ("attn_o1", [P, 2, 384], F32),
        ("attn_ones", [3, P], BF16), ("attn_mean", [P, TB], F32), ("attn_rstd", [P, TB], F32),
        ("attn_tmp", [P, TB], F32), ("attn_dev", [P, TB, 2], F32), ("attn_stats", [P, TB, 6], F32),
        ("attn_z", [P, 6], F32), ("attn_den", [P, 6], F32))
    bgrows = K.attn_bgrows
    AB, OB, TF, TH = 32, 24, 32, 24

    def t_fill(b, u, k):
        return 8 + TF * b + 8 * (u - 1) + k

    def t_hi(b, u, k):
        return 8 + TH * b + 6 * (u - 1) + k

    with nc.Block() as block:

        @block.sync
        def _(sp):
            for dst, src in K.ffn_consts:
                sp.dma_start(dst, src, allow_slow_non_contiguous=True).then_inc(s.consts_in.sem, 16)
            sp.wait_ge(*s.zeroed.after(1))
            sp.dma_start(A.scratch[0:1, :], K.zrow[:]).then_inc(s.consts_in.sem, 16)
            sp.wait_ge(*s.consts_in.after(16 * (len(K.ffn_consts) + 1)))

        @block.gpsimd
        def _(pool):
            nc.gpsimd.memset(K.zrow[:], 0.0).then_inc(s.zeroed.sem, 1)
            nc.gpsimd.memset(ones[:], 1.0)
            nc.gpsimd.memset(vs[:, :, :, P:VC], 1.0)
            nc.gpsimd.memset(kv[:], 0.0).then_inc(s.attn_set.sem, 1)
            pool.wait_ge(*s.attn_wo_hi.after(1))
            nc.gpsimd.tensor_tensor(wol[:], woraw[:], f32(woh[:]), ALU.subtract).then_inc(s.attn_wo_lo.sem, 1)

        @block.scalar
        def _(act):
            nc.scalar.activation(woh[:], woraw[:], ACT.Copy).then_inc(s.attn_wo_hi.sem, 1)

            def xt_hi(t_bank, tile, hi_n, full_n):
                act.wait_ge(*s.attn_t_full.after(full_n + 1))
                nc.scalar.activation(xth[:, :, tile * P:(tile + 1) * P],
                                     ps[:, t_bank, 0:D].rearrange("p (c t) -> p c t", c=KC),
                                     ACT.Copy).then_inc(s.attn_t_hi.sem, 1)

            for j in range(TB):
                xt_hi(6 + j % 2, j, j, j)

            def exp_(n, at):
                act.wait_ge(*s.attn_a_full.after(n + 1))
                act.wait_ge(*s.attn_feat.room(n, 2))
                nc.scalar.activation(ex[:, at % 2], ps[:, at % 2], ACT.Exp).then_inc(s.attn_exp.sem, 1)

            def tanh_(b, n):
                act.wait_ge(*s.attn_o.after(OB * b + 3 * (n - 1)))
                for half in range(2):
                    act.wait_ge(*s.attn_b_full.after(AB * b + 16 + 2 * n + half + 1))
                    nc.scalar.activation(th[:, n % 2, half * HALF:(half + 1) * HALF], ps[:, 2 + half],
                                         ACT.Tanh, scale=0.5).then_inc(s.attn_b_done.sem, 1)

            def ot_hi(b, u, which):
                act.wait_ge(*s.attn_t_full.after(t_fill(b, u, 2) if which else t_fill(b, u, -3)))
                for half in range(2):
                    k = 3 * which + half
                    act.wait_ge(*s.attn_t_full.after(t_fill(b, u, k) + 1))
                    nc.scalar.activation(oth[:, 4 * half:4 * half + 4, :].rearrange("p c t -> p (c t)"),
                                         ps[:, 6 + k % 2], ACT.Copy).then_inc(s.attn_t_hi.sem, 1)

            with act.Fori(0, B) as b:
                for j in range(TB):
                    for half in range(2):
                        exp_(AB * b + 2 * j + half, half)
                    act.wait_ge(*s.attn_kv_mm.room(TB * b + j, 2))
                    for half in range(2):
                        act.wait_ge(*s.attn_b_full.after(AB * b + 2 * j + half + 1))
                        nc.scalar.activation(vs[:, j % 2, 4 * half:4 * half + 4, 0:P],
                                             ps[:, 2 + half].rearrange("p (m c) -> p m c", m=4),
                                             ACT.Copy).then_inc(s.attn_b_done.sem, 1)
                for u in range(TB // 2):
                    for f in range(2):
                        exp_(AB * b + 16 + 4 * u + f, f)
                    if u:
                        ot_hi(b, u, 0)
                    for f in range(2, 4):
                        exp_(AB * b + 16 + 4 * u + f, f)
                    tanh_(b, 2 * u)
                    if u:
                        ot_hi(b, u, 1)
                    tanh_(b, 2 * u + 1)
                    if u:
                        for w in range(2):
                            xt_hi(6 + w, 2 * u - 2 + w, t_hi(b, u, 4 + w), t_fill(b, u, 6 + w))
                u = TB // 2
                ot_hi(b, u, 0)
                ot_hi(b, u, 1)
                for w in range(2):
                    xt_hi(6 + w, 2 * u - 2 + w, t_hi(b, u, 4 + w), t_fill(b, u, 6 + w))

        @block.vector
        def _(dve):
            chain = Chain(dve, s.attn_dve.sem)

            def stats(tile, j):
                return nc.vector.bn_stats(st[:, j, :], H[:, tile, :])

            norm = Stats(st[:], TB, 2, mean[:], rs[:], tmp[:], dev[:])

            def normalise(tile, j):
                nc.vector.tensor_scalar(xn[:, j % 2], H[:, tile, :], mean[:, j:j + 1], rs[:, j:j + 1],
                                        ALU.subtract, ALU.mult).then_inc(s.attn_xn.sem, 1)

            def xt_lo(t_bank, tile, hi_n):
                dve.wait_ge(*s.attn_t_hi.after(hi_n + 1))
                cols = slice(tile * P, (tile + 1) * P)
                nc.vector.tensor_tensor(xtl[:, :, cols], ps[:, t_bank, 0:D].rearrange("p (c t) -> p c t", c=KC),
                                        f32(xth[:, :, cols]), ALU.subtract).then_inc(s.attn_t_done.sem, 1)

            for j in range(TB):
                last = stats(j, j)
            chain(last)
            norm.finish(nc, chain)
            for j in range(TB):
                if j >= 2:
                    dve.wait_ge(*s.attn_t_full.after(j - 1))
                normalise(j, j)
                if j:
                    xt_lo(6 + (j - 1) % 2, j - 1, j - 1)
            xt_lo(6 + (TB - 1) % 2, TB - 1, TB - 1)

            def feature(n, at, dst):
                dve.wait_ge(*s.attn_exp.after(n + 1))
                chain(nc.vector.tensor_scalar(ex[:, at % 2], ex[:, at % 2], 1.0, None, ALU.min))
                src, e = ps[:, at % 2], ex[:, at % 2]
                if len(dst.shape) == 3:
                    src, e = (v.rearrange("p (m t) -> p m t", m=2) for v in (src, e))
                nc.vector.scalar_tensor_tensor(dst, src, 0.0, e, ALU.max, ALU.add).then_inc(s.attn_feat.sem, 1)

            def ot_lo(b, u, which):
                for half in range(2):
                    dve.wait_ge(*s.attn_t_hi.after(t_hi(b, u, 2 * which + half) + 1))
                    m = slice(4 * half, 4 * half + 4)
                    nc.vector.tensor_tensor(otl[:, m, :].rearrange("p c t -> p (c t)"), ps[:, 6 + (3 * which + half) % 2],
                                            f32(oth[:, m, :].rearrange("p c t -> p (c t)")),
                                            ALU.subtract).then_inc(s.attn_t_done.sem, 1)

            def residual(b, u, which):
                dve.wait_ge(*s.attn_t_full.after(t_fill(b, u, 3 * which + 2) + 1))
                tile = H[:, bass.ds(TB * b + 2 * u - 2 + which, 1), :]
                nc.vector.tensor_tensor(tile, ps[:, 6 + which % 2:7 + which % 2, 0:D], tile, ALU.add).then_inc(s.attn_t_done.sem, 1)

            def gated(b, n):
                for g, (m0, m1) in enumerate(GROUPS):
                    w = m1 - m0
                    dve.wait_ge(*s.attn_o_full.after(OB * b + 3 * n + g + 1))
                    out = ps[:, 4 + (3 * n + g) % 2, 0:w * OC].rearrange("p (m c) -> p m c", c=OC)
                    chain(nc.vector.tensor_scalar(zd[:, 0:2 * w].rearrange("p (m e) -> p m e", e=2), out[:, :, P:OC],
                                                  1e-6, 2.0 * DH ** 0.5, ALU.max, ALU.mult))
                    chain(nc.vector.reciprocal(z[:, 0:2 * w], zd[:, 0:2 * w]))
                    zb = z[:, 0:2 * w].rearrange("p (m e) -> p m e", e=2).unsqueeze(3).to_broadcast([P, w, 2, DH])
                    chain(nc.vector.tensor_tensor(o1[:, g % 2, 0:w * P].rearrange("p (m e d) -> p m e d", e=2, d=DH),
                                                  out[:, :, 0:P].rearrange("p m (e d) -> p m e d", e=2), zb, ALU.mult))
                    if g == 0:
                        dve.wait_ge(*s.attn_b_done.after(AB * b + 16 + 2 * n + 2))
                    nc.vector.scalar_tensor_tensor(og[:, n % 2, m0 * P:m1 * P], th[:, n % 2, m0 * P:m1 * P], 1.0,
                                                   o1[:, g % 2, 0:w * P], ALU.add, ALU.mult).then_inc(s.attn_o.sem, 1)

            PER_BATCH = 2 * TB + 4 * (TB // 2) + 1 + STATS_STEPS + 3 * len(GROUPS) * TB
            start = chain.n
            dve.wait_ge(*s.attn_set.after(1))
            with dve.Fori(0, B) as b:
                chain.rebase(start + PER_BATCH * b)
                dve.wait_ge(*s.attn_t_done.after(t_fill(b, 1, 0)))
                nxt = TB * ((b + 1) % B)
                for j in range(TB):
                    for half in range(2):
                        feature(AB * b + 2 * j + half, half, ks[:, j % 2, half * HALF:(half + 1) * HALF])
                    last = stats(bass.ds(nxt + j, 1), j)
                chain(last)
                norm.finish(nc, chain)
                dve.wait_ge(*s.attn_kv_mm.after(TB * b + TB))
                for g, (m0, m1) in enumerate(GROUPS):
                    acc = ps[:, 4 + g, 0:(m1 - m0) * VC].rearrange("p (m c) -> p m c", c=VC)
                    for e in range(2):
                        r = slice(e * DH, (e + 1) * DH)
                        nc.vector.tensor_copy(kv[r, m0:m1, e * DH:(e + 1) * DH], acc[r, :, e * DH:(e + 1) * DH])
                        last = nc.vector.tensor_copy(kv[r, m0:m1, P + e:P + e + 1], acc[r, :, P:VC])
                last.then_inc(s.attn_kv.sem, 1)
                for u in range(TB // 2 + 1):
                    if u:
                        for w in range(2):
                            normalise(bass.ds(nxt + 2 * u - 2 + w, 1), 2 * u - 2 + w)
                    if u < TB // 2:
                        for f in range(2):
                            feature(AB * b + 16 + 4 * u + f, f, qt[:, 2 * f:2 * f + 2, :])
                    if u:
                        ot_lo(b, u, 0)
                    if u < TB // 2:
                        for f in range(2, 4):
                            feature(AB * b + 16 + 4 * u + f, f, qt[:, 2 * f:2 * f + 2, :])
                    if u:
                        residual(b, u, 0)
                        ot_lo(b, u, 1)
                        residual(b, u, 1)
                        for w in range(2):
                            xt_lo(6 + w, 2 * u - 2 + w, t_hi(b, u, 4 + w))
                    if u < TB // 2:
                        gated(b, 2 * u)
                        gated(b, 2 * u + 1)
                assert chain.n == PER_BATCH, (chain.n, PER_BATCH)

        @block.tensor
        def _(pe):
            def xt(bank, xn_n, slot, fill_n):
                pe.wait_ge(*s.attn_xn.after(xn_n + 1))
                pe.wait_ge(*s.attn_t_done.room(fill_n, 2))
                for c in range(KC):
                    last = nc.tensor.transpose(ps[:, bank, c * P:(c + 1) * P], xn[:, slot, c * P:(c + 1) * P], K.ident[:])
                last.then_inc(s.attn_t_full.sem, 1)

            for j in range(TB):
                xt(6 + j % 2, j, j % 2, j)

            def rows(w, n, tile, bank0, full, free, count, bias):
                for half in range(2):
                    cols = slice(half * HALF, (half + 1) * HALF)
                    out = ps[:, bank0 + half]
                    pe.wait_ge(*free.room(count + half, 2))
                    if bias:
                        nc.tensor.matmul(out, ones[:], bgrows[:, cols], start=True, stop=False, skip_group_check=True)
                    for c in range(KC):
                        t = slice(tile * P, (tile + 1) * P)
                        last = matmul3(nc, out, xth[:, c, t], xtl[:, c, t], wh[:, w, c, cols], wl[:, w, c, cols],
                                       c == 0 and not bias, c == KC - 1)
                    last.then_inc(full.sem, 1)

            def kv_products(b, j):
                pe.wait_ge(*s.attn_feat.after(AB * b + 2 * j + 2))
                pe.wait_ge(*s.attn_b_done.after(AB * b + 2 * j + 2))
                for g, (m0, m1) in enumerate(GROUPS):
                    for m in range(m0, m1):
                        last = nc.tensor.matmul(ps[:, 4 + g, (m - m0) * VC:(m - m0 + 1) * VC],
                                                ks[:, j % 2, m * P:(m + 1) * P], vs[:, j % 2, m, :],
                                                start=(j == 0 and m == m0), stop=(j == TB - 1),
                                                skip_group_check=True)
                last.then_inc(s.attn_kv_mm.sem, 1)

            def queries(b, u, f):
                n = AB * b + 16 + 4 * u + f
                pe.wait_ge(*s.attn_feat.room(n, 2))
                for i in range(2):
                    m = 2 * f + i
                    for c in range(KC):
                        t = slice(2 * u * P, (2 * u + 2) * P)
                        last = matmul3(nc, ps[:, f % 2, i * 2 * P:(i + 1) * 2 * P], wh[:, Q, c, m * P:(m + 1) * P],
                                       wl[:, Q, c, m * P:(m + 1) * P], xth[:, c, t], xtl[:, c, t],
                                       c == 0, c == KC - 1)
                last.then_inc(s.attn_a_full.sem, 1)

            def outputs(b, u, which):
                n = 2 * u + which
                pe.wait_ge(*s.attn_feat.after(AB * b + 16 + 4 * u + 4))
                pe.wait_ge(*s.attn_kv.after(b + 1))
                for g, (m0, m1) in enumerate(GROUPS):
                    pe.wait_ge(*s.attn_o.room(OB * b + 3 * n + g, 2))
                    for m in range(m0, m1):
                        last = nc.tensor.matmul(ps[:, 4 + (3 * n + g) % 2, (m - m0) * OC:(m - m0 + 1) * OC],
                                                qt[:, m, which * P:(which + 1) * P], kv[:, m, :],
                                                start=True, stop=True)
                    last.then_inc(s.attn_o_full.sem, 1)

            def out_transposes(b, u, which):
                n = 2 * (u - 1) + which
                pe.wait_ge(*s.attn_o.after(OB * b + 3 * n + 3))
                for half in range(2):
                    k = 3 * which + half
                    pe.wait_ge(*s.attn_t_done.room(t_fill(b, u, k), 2))
                    for i in range(4):
                        m = 4 * half + i
                        last = nc.tensor.transpose(ps[:, 6 + k % 2, i * P:(i + 1) * P],
                                                   og[:, which, m * P:(m + 1) * P], K.ident[:])
                    last.then_inc(s.attn_t_full.sem, 1)

            def out_products(b, u, which):
                k = 3 * which + 2
                pe.wait_ge(*s.attn_t_done.after(t_fill(b, u, k)))
                for m in range(PAIRS):
                    last = matmul3(nc, ps[:, 6 + k % 2, 0:D], oth[:, m, :], otl[:, m, :], woh[:, m, :], wol[:, m, :],
                                   m == 0, m == PAIRS - 1)
                last.then_inc(s.attn_t_full.sem, 1)

            pe.wait_ge(*s.attn_set.after(1))
            with pe.Fori(0, B) as b:
                pe.wait_ge(*s.attn_t_done.after(t_fill(b, 1, 0)))
                for j in range(TB):
                    rows(KEY, AB * b + 2 * j, j, 0, s.attn_a_full, s.attn_feat, AB * b + 2 * j, False)
                    rows(VAL, AB * b + 2 * j, j, 2, s.attn_b_full, s.attn_b_done, AB * b + 2 * j, False)
                    if j == 1:
                        pe.wait_ge(*s.attn_o.after(OB * b))
                    if j:
                        kv_products(b, j - 1)
                kv_products(b, TB - 1)
                pe.wait_ge(*s.attn_wo_lo.after(1))
                for u in range(TB // 2 + 1):
                    if u < TB // 2:
                        queries(b, u, 0)
                        queries(b, u, 1)
                    if u:
                        out_transposes(b, u, 0)
                    if u < TB // 2:
                        queries(b, u, 2)
                        queries(b, u, 3)
                    if u:
                        out_products(b, u, 0)
                    if u < TB // 2:
                        count = AB * b + 16 + 4 * u
                        rows(GATE, count, 2 * u, 2, s.attn_b_full, s.attn_b_done, count, True)
                    if u:
                        out_transposes(b, u, 1)
                    if u < TB // 2:
                        rows(GATE, count + 2, 2 * u + 1, 2, s.attn_b_full, s.attn_b_done, count + 2, True)
                    if u:
                        out_products(b, u, 1)
                        for w in range(2):
                            xt(6 + w, TB * (b + 1) + 2 * u - 2 + w, w, t_fill(b, u, 6 + w))
                    if u < TB // 2:
                        outputs(b, u, 0)
                        outputs(b, u, 1)



def wait(eng, count, n):
    if not isinstance(n, int) or n > 0:
        eng.wait_ge(*count.after(n))


def local_phase(nc, s, mem, K, A, layer):
    ps, X = K.ps, K.X
    wh, wl, wraw, woh, wol, woraw = K.qkv_h, K.qkv_l, K.qkv_raw, K.wo_h, K.wo_l, K.wo_raw
    XW = P + 2
    (idle, xc, xt, sq, t1, t2, rot, qt, kt, vv, pm, pt, osb, oth, otl, cos, sin, mask_e, mask_o, prev, flags, negs, qks,
     ss, rn, tmp, mx, nb, rsum, rinv, mean, rs, st, tmp32, dev), _ = mem.place(
        K.mlp_end, mem.end,
        (f"l{layer}_idle", [P, 1], F32), (f"l{layer}_x", [P, 2, D], F32), (f"l{layer}_xT", [P, 2, 2, 2 * XW], F32R), (f"l{layer}_sq", [P, 2, LINNER], F32),
        (f"l{layer}_t1", [P, 2, LINNER], F32), (f"l{layer}_t2", [P, 2, LINNER], F32),
        (f"l{layer}_rot", [P, 2, LINNER], F32), (f"l{layer}_qT", [P, LPAIRS, P], F32),
        (f"l{layer}_kT", [P, 2, LPAIRS, P], F32), (f"l{layer}_v", [P, 2, LINNER], F32),
        (f"l{layer}_probs", [P, LPAIRS, 4 * P], F32), (f"l{layer}_probsT", [P, 2, 4 * P], F32),
        (f"l{layer}_o", [P, LINNER], F32), (f"l{layer}_oT_hi", [P, LINNER], F32R),
        (f"l{layer}_oT_lo", [P, LINNER], F32R), (f"l{layer}_cos", [P, TB, 2, DH], F32),
        (f"l{layer}_sin", [P, TB, 2, DH], F32), (f"l{layer}_mask_even", [P, 2 * P], F32),
        (f"l{layer}_mask_odd", [P, 2 * P], F32), (f"l{layer}_mask_prev", [P, P], F32),
        (f"l{layer}_flags", [P, T // 2], F32), (f"l{layer}_negs", [P, T // 2], F32),
        (f"l{layer}_qkscale", [P, 2, DH], F32), (f"l{layer}_ss", [P, 2 * LH], F32),
        (f"l{layer}_rnorm", [P, 2 * LH], F32), (f"l{layer}_tmp", [P, 2 * LH], F32),
        (f"l{layer}_max", [P, LH], F32), (f"l{layer}_negmax", [P, LH], F32), (f"l{layer}_rowsum", [P, LH], F32),
        (f"l{layer}_rowinv", [P, LH], F32), (f"l{layer}_mean", [P, T], F32),
        (f"l{layer}_rstd", [P, T], F32), (f"l{layer}_stats", [P, T, 6], F32),
        (f"l{layer}_tmp32", [P, T], F32), (f"l{layer}_dev", [P, T, 2], F32))

    def schedule(eng, step, rebase=None):
        for n in (0, 1):
            rebase and rebase(None)
            step(n, n, True, n >= 1, False)
        with eng.Fori(1, T // 2) as p:
            rebase and rebase(p - 1)
            for r in range(2):
                step(2 * p + r, r, True, True, True)
        rebase and rebase(T // 2 - 1)
        step(T, 0, False, True, True)
        step(T + 1, 1, False, False, True)

    def turn(r, k):
        return 5 + (r + k) % 2

    OT, Y, XT = 0, 1, 4
    PT = (2, 3, 5, 6)

    with nc.Block() as block:

        @block.sync
        def _(sp):
            for dst, src in ((cos[:], A.rope_cos), (sin[:], A.rope_sin), (prev[:], A.mask_prev),
                             (mask_o[:, P:2 * P], A.mask_cur), (mask_e[:, 0:P], A.mask_cur),
                             (mask_o[:, 0:P], A.mask_prev), (flags[:], A.flags), (negs[:], A.negs),
                             (qks[:, 0, :], A.ffn_q_scale[layer:layer + 1].to_broadcast([P, DH])),
                             (qks[:, 1, :], A.ffn_k_scale[layer:layer + 1].to_broadcast([P, DH]))):
                sp.dma_start(dst, src).then_inc(s.const_in.sem, 16)
            if layer == 0:
                for dst, src in K.local_loads(layer):
                    sp.dma_start(dst, src).then_inc(K.local_in.sem, 16)
            sp.wait_ge(*s.padded.after(1))
            for dst, src in K.mlp_loads(layer):
                sp.dma_start(dst, src).then_inc(K.mlp_in.sem, 16)
            with sp.Fori(0, T // 2) as p:
                for r in range(2):
                    sp.wait_ge(*s.y_done.after(2 * p + r + 1))
                    sp.dma_start(A.scratch[bass.ds((2 * p + r) * P + 1, P), :].rearrange("(o p) c -> p o c", o=1),
                                 X[:, bass.ds(2 * p + r, 1), P:D]).then_inc(s.stored[r].sem, 16)
            for r in range(2):
                sp.wait_ge(*s.stored[r].after(16 * (T // 2)))
            sp.wait_ge(*K.mlp_in.after(16 * len(K.mlp_loads(layer)) * (layer + 1)))

        @block.gpsimd
        def _(pool):
            nc.gpsimd.memset(K.w1_raw[:, :, 2 * HC * P + HR:2 * HC * P + GR], 0.0)
            nc.gpsimd.memset(K.w2_raw[:, HC, :], 0.0).then_inc(s.padded.sem, 1)
            nc.gpsimd.memset(kt[:, 1], 0.0)
            nc.gpsimd.memset(vv[:, 1], 0.0)
            nc.gpsimd.memset(xt[:, 1].bitcast(F32), 0.0).then_inc(s.set.sem, 1)
            with pool.Fori(0, T) as t:
                pool.wait_ge(*s.turned.after(t + 1))
                pool.wait_ge(*s.qk_t.after(2 * t))
                nc.gpsimd.tensor_tensor(rot[:], t1[:], t2[:], ALU.add).then_inc(s.summed.sem, 1)
                pool.wait_ge(*s.summed.after(t + 1))
                pool.wait_ge(*s.rnorm.after(t + 1))
                r = rot[:].rearrange("p a (h d) -> p (a h) d", d=DH)
                nc.gpsimd.tensor_tensor(r, r, rn[:].unsqueeze(2).to_broadcast([P, 2 * LH, DH]),
                                        ALU.mult).then_inc(s.rotated.sem, 1)

        @block.scalar
        def _(act):
            act.wait_ge(*K.local_in.after(16 * len(K.local_loads(layer)) * (layer + 1)))
            for h, raw in ((wh, wraw), (woh, woraw)):
                nc.scalar.activation(h[:], raw[:], ACT.Copy).then_inc(s.w_hi.sem, 1)

            def x_hi(t, r, bank):
                wait(act, s.x_t, t + 1)
                nc.scalar.activation(xt[:, r, 0, :].rearrange("p (c w) -> p c w", w=XW)[:, :, 0:P],
                                     ps[:, bank, 0:D].rearrange("p (c w) -> p c w", c=KC),
                                     ACT.Copy).then_inc(s.x_hi.sem, 1)

            def exps(t, pair):
                wait(act, s.negmax, 2 * t + pair // 2 + 1)
                for e in range(2):
                    h = 2 * pair + e
                    v = pm[:, pair, e * 2 * P:(e + 1) * 2 * P]
                    last = nc.scalar.activation(v, v, ACT.Exp, bias=nb[:, h:h + 1], scale=8.0,
                                                accum_out=rsum[:, h:h + 1])
                last.then_inc(s.exped.sem, 1)

            def probs_out(t, pair, r):
                wait(act, s.p_t, 4 * t + pair + 1)
                nc.scalar.activation(pt[:, pair % 2], ps[:, turn(r, PT[pair])], ACT.Copy).then_inc(s.p_done.sem, 1)

            def step(n, r, a, b, c):
                if a:
                    wait(act, s.qk_full, n + 1)
                    wait(act, s.rnorm, n)
                    nc.scalar.activation(sq[:], ps[:, 0:2], ACT.Square).then_inc(s.squared.sem, 1)
                if c:
                    wait(act, s.o_t, n - 1)
                    nc.scalar.activation(oth[:], ps[:, turn(r, OT)], ACT.Copy).then_inc(s.o_hi.sem, 1)
                if b:
                    for k, dst in enumerate((qt[:], kt[:, 1 - r])):
                        wait(act, s.qk_t, 2 * (n - 1) + k + 1)
                        nc.scalar.activation(dst.rearrange("p m t -> p (m t)"), ps[:, 3 + k],
                                             ACT.Copy).then_inc(s.qk_done.sem, 1)
                    exps(n - 1, 0)
                    exps(n - 1, 1)
                    probs_out(n - 1, 0, r)
                    probs_out(n - 1, 1, r)
                if a:
                    x_hi(n + 1, 1 - r, turn(r, XT))
                if b:
                    exps(n - 1, 2)
                    exps(n - 1, 3)
                    probs_out(n - 1, 2, r)
                    probs_out(n - 1, 3, r)
                if a:
                    wait(act, s.v_full, n + 1)
                    wait(act, s.o_full, n)
                    nc.scalar.activation(vv[:, r], ps[:, 2], ACT.Copy).then_inc(s.v_done.sem, 1)

            x_hi(0, 0, turn(1, XT))
            schedule(act, step)

        @block.vector
        def _(dve):
            chain = Chain(dve, s.dve.sem)
            if layer == 0:
                for t in range(T):
                    last = nc.vector.bn_stats(st[:, t, :], K.H[:, t, :])
                chain(last)
                Stats(st[:], T, 2, mean[:], rs[:], tmp32[:], dev[:]).finish(nc, chain)
            for k, (lo, raw, hi) in enumerate(((wl, wraw, wh), (wol, woraw, woh))):
                dve.wait_ge(*s.w_hi.after(k + 1))
                nc.vector.tensor_tensor(lo[:], raw[:], f32(hi[:]), ALU.subtract).then_inc(s.w_lo.sem, 1)
            dve.wait_ge(*s.const_in.after(160))
            nc.vector.tensor_tensor(cos[:], cos[:], qks[:].unsqueeze(1).to_broadcast([P, TB, 2, DH]), ALU.mult)
            HF = DH // 2
            for e in range(2):
                last = nc.vector.tensor_tensor(sin[:, :, :, e * HF:(e + 1) * HF], sin[:, :, :, e * HF:(e + 1) * HF],
                                               qks[:, :, (1 - e) * HF:(2 - e) * HF].unsqueeze(1)
                                               .to_broadcast([P, TB, 2, HF]), ALU.mult)
            chain(last)
            dve.wait_ge(*s.set.after(1))

            def x_lo(t, r, bank):
                wait(dve, s.x_hi, t + 1)
                hi, lo = (xt[:, r, k, :].rearrange("p (c w) -> p c w", w=XW)[:, :, 0:P] for k in (0, 1))
                chain(nc.vector.tensor_tensor(lo, ps[:, bank, 0:D].rearrange("p (c w) -> p c w", c=KC), f32(hi),
                                              ALU.subtract))
                flag = 1.0 if r else flags[:, bass.ds(t // 2 if isinstance(t, int) else x_lo.pair, 1)]
                nc.vector.tensor_scalar(xt[:, r, :, XW - 1:XW], f32(xt[:, 1 - r, :, 2 * XW - 3:2 * XW - 2]), flag, None,
                                        ALU.mult).then_inc(s.x_done.sem, 1)

            def scores(t, half, mask):
                wait(dve, s.scored, 2 * t + half + 1)
                nc.vector.memset(idle[:], 0.0)
                for h in range(4 * half, 4 * half + 4):
                    pair, e, at = h // 2, h % 2, h // 2 % 2 * 2 * P
                    last = nc.vector.tensor_tensor_reduce(
                        pm[:, pair, e * 2 * P:(e + 1) * 2 * P], ps[:, 3 + e, at:at + 2 * P],
                        mask[:], 1.0, LOWEST, ALU.add, ALU.max, mx[:, h:h + 1])
                last.then_inc(s.masked.sem, 1)
                wait(dve, s.masked, 2 * t + half + 1)
                h = slice(4 * half, 4 * half + 4)
                nc.vector.tensor_scalar(nb[:, h], mx[:, h], -8.0, None, ALU.mult).then_inc(s.negmax.sem, 1)

            def normalise(dst, t):
                tile = bass.ds(t, 1)
                return nc.vector.tensor_scalar(dst, K.H[:, tile], mean[:, tile], rs[:, tile], ALU.subtract, ALU.mult)

            def x_copy(t, r):
                tile = bass.ds(t, 1)
                if layer == 0:
                    last = normalise(xc[:, r:r + 1], t)
                else:
                    last = nc.vector.tensor_scalar(xc[:, r:r + 1], X[:, tile], 1.0, None, ALU.mult)
                last.then_inc(s.x_copied.sem, 1)

            def step(n, r, a, b, c):
                if a:
                    x_copy((n + 1) % T, 1 - r)
                    if layer == 0:
                        normalise(X[:, bass.ds(n, 1)], n)
                mask = mask_o if r == 0 else mask_e
                if b and r == 1:
                    p = (n - 1) // 2 if isinstance(n, int) else step.pair
                    chain(nc.vector.tensor_scalar(mask_e[:, P:2 * P], prev[:], negs[:, bass.ds(p, 1)], None, ALU.add))
                if a:
                    wait(dve, s.squared, n + 1)
                    wait(dve, s.summed, n)
                    w = bass.ds(n % TB, 1)
                    q = ps[:, 0:2].rearrange("p a (h d) -> p a h d", d=DH)
                    cw = cos[:, w].rearrange("p o a d -> p a o d").to_broadcast([P, 2, LH, DH])
                    nc.vector.tensor_tensor(t1[:].rearrange("p a (h d) -> p a h d", d=DH), q, cw, ALU.mult)
                    t2v = t2[:].rearrange("p a (h d) -> p a h d", d=DH)
                    for e in range(2):
                        here, there = slice(e * HF, (e + 1) * HF), slice((1 - e) * HF, (2 - e) * HF)
                        sw = sin[:, w, :, here].rearrange("p o a d -> p a o d").to_broadcast([P, 2, LH, HF])
                        last = nc.vector.tensor_tensor(t2v[:, :, :, here], q[:, :, :, there], sw, ALU.mult)
                    last.then_inc(s.turned.sem, 1)
                if c:
                    wait(dve, s.o_hi, n - 1)
                    nc.vector.tensor_tensor(otl[:], ps[:, turn(r, OT)], f32(oth[:]), ALU.subtract).then_inc(s.o_done.sem, 1)
                if b:
                    scores(n - 1, 0, mask)
                if c:
                    wait(dve, s.y_full, n - 1)
                    tile = X[:, bass.ds(n - 2, 1), :]
                    nc.vector.tensor_tensor(tile, ps[:, turn(r, Y):turn(r, Y) + 1, 0:D], tile, ALU.add).then_inc(s.y_done.sem, 1)
                if a:
                    chain(nc.vector.tensor_reduce(ss[:], sq[:].rearrange("p a (h d) -> p (a h) d", d=DH), AX.X, ALU.add))
                if b:
                    scores(n - 1, 1, mask)
                if a:
                    x_lo(n + 1, 1 - r, turn(r, XT))
                    wait(dve, s.rotated, n)
                    chain(nc.vector.tensor_scalar(ss[:], ss[:], 1e-24, None, ALU.max))
                    rsqrt(nc, chain, rn[:], tmp[:], ss[:])
                    dve.sem_inc(s.rnorm.sem, 1)
                if b:
                    wait(dve, s.o_full, n)
                    chain(nc.vector.reciprocal(rinv[:], rsum[:]))
                    nc.vector.tensor_tensor(osb[:].rearrange("p (h d) -> p h d", d=DH),
                                            ps[:, 7].rearrange("p (h d) -> p h d", d=DH),
                                            rinv[:].unsqueeze(2).to_broadcast([P, LH, DH]), ALU.mult).then_inc(s.o_norm.sem, 1)

            x_copy(0, 0)
            x_lo(0, 0, turn(1, XT))
            marks = []

            def rebase(p):
                if p is None:
                    chain.rebase(chain.base + chain.n)
                elif isinstance(p, int):
                    assert 2 * chain.n == 2 * PER_PAIR, (chain.n, PER_PAIR)
                    chain.rebase(marks[0] + PER_PAIR * p)
                else:
                    marks.append(chain.base + chain.n)
                    chain.rebase(marks[0] + PER_PAIR * p)
                    step.pair = p + 1
                    x_lo.pair = p + 2 - (p + 2) // (T // 2) * (T // 2) if isinstance(p, int) else (p + 2) % (T // 2)

            PER_PAIR = 1 + 2 * (12 + 1 + 1)
            schedule(dve, step, rebase)

        @block.tensor
        def _(pe):
            def x_t(t, r, bank):
                wait(pe, s.x_copied, t + 1)
                for c in range(KC):
                    last = nc.tensor.transpose(ps[:, bank, c * P:(c + 1) * P],
                                               xc[:, r, c * P:(c + 1) * P], K.ident[:])
                last.then_inc(s.x_t.sem, 1)

            def project(n, r, w, bank):
                cols = slice(w * LINNER, (w + 1) * LINNER)
                for c in range(KC):
                    at = XW * c - c
                    last = matmul3(nc, ps[:, bank], xt[:, r, 0, at:at + P], xt[:, r, 1, at:at + P],
                                   wh[:, c, cols], wl[:, c, cols], c == 0, c == KC - 1)
                return last

            def score(t, half):
                for pair in (2 * half, 2 * half + 1):
                    for e in range(2):
                        rows, at = slice(e * DH, (e + 1) * DH), pair % 2 * 2 * P
                        last = nc.tensor.matmul(ps[:, 3 + e, at:at + 2 * P], qt[rows, pair, :],
                                                kt[rows, :, pair, :], start=True, stop=True)
                last.then_inc(s.scored.sem, 1)

            def probs_t(t, pair, r):
                wait(pe, s.exped, 4 * t + pair + 1)
                for k in range(4):
                    last = nc.tensor.transpose(ps[:, turn(r, PT[pair]), k * P:(k + 1) * P],
                                               pm[:, pair, k * P:(k + 1) * P], K.ident[:])
                last.then_inc(s.p_t.sem, 1)

            def values(t, pair):
                wait(pe, s.p_done, 4 * t + pair + 1)
                for e in range(2):
                    h = 2 * pair + e
                    for w in range(2):
                        last = nc.tensor.matmul(ps[:, 7, h * DH:(h + 1) * DH],
                                                pt[:, pair % 2, (2 * e + w) * P:(2 * e + w + 1) * P],
                                                vv[:, w, h * DH:(h + 1) * DH], start=(w == 0), stop=(w == 1))
                if pair == LPAIRS - 1:
                    last.then_inc(s.o_full.sem, 1)

            def step(n, r, a, b, c):
                t = n - 1
                if a:
                    wait(pe, s.x_done, n + 1)
                    wait(pe, s.turned, n)
                    project(n, r, 0, 0)
                    project(n, r, 1, 1).then_inc(s.qk_full.sem, 1)
                if c:
                    wait(pe, s.o_norm, n - 1)
                    for m in range(LPAIRS):
                        last = nc.tensor.transpose(ps[:, turn(r, OT), m * P:(m + 1) * P], osb[:, m * P:(m + 1) * P],
                                                   K.ident[:])
                    last.then_inc(s.o_t.sem, 1)
                if b:
                    wait(pe, s.rotated, n)
                    wait(pe, s.masked, 2 * t)
                    for k in range(2):
                        for m in range(LPAIRS):
                            last = nc.tensor.transpose(ps[:, 3 + k, m * P:(m + 1) * P], rot[:, k, m * P:(m + 1) * P],
                                                       K.ident[:])
                        last.then_inc(s.qk_t.sem, 1)
                if a:
                    wait(pe, s.v_done, n)
                    project(n, r, 2, 2).then_inc(s.v_full.sem, 1)
                if b:
                    wait(pe, s.qk_done, 2 * n)
                    score(t, 0)
                if c:
                    wait(pe, s.o_done, n - 1)
                    for m in range(LPAIRS):
                        cols = slice(m * P, (m + 1) * P)
                        last = matmul3(nc, ps[:, turn(r, Y), 0:D], oth[:, cols], otl[:, cols], woh[:, m, :], wol[:, m, :],
                                       m == 0, m == LPAIRS - 1)
                    last.then_inc(s.y_full.sem, 1)
                if b:
                    wait(pe, s.masked, 2 * t + 1)
                    score(t, 1)
                    probs_t(t, 0, r)
                    if c:
                        wait(pe, s.y_done, n - 1)
                    probs_t(t, 1, r)
                if a:
                    wait(pe, s.p_done, 4 * t + 1)
                    x_t(n + 1, 1 - r, turn(r, XT))
                if b:
                    wait(pe, s.o_norm, t)
                    values(t, 0)
                    values(t, 1)
                    probs_t(t, 2, r)
                    if a:
                        wait(pe, s.x_done, n + 2)
                    probs_t(t, 3, r)
                    values(t, 2)
                    values(t, 3)

            x_t(0, 0, turn(1, XT))
            pe.wait_ge(*s.w_lo.after(2))
            schedule(pe, step)


def mlp_phase(nc, s, mem, K, A, layer, last_layer):
    ps, X = K.ps, K.X
    w1h, w1l, w1raw, w2h, w2l, w2raw = K.w1_h, K.w1_l, K.w1_raw, K.w2_h, K.w2_l, K.w2_raw
    G = 4
    GT = G * P
    NG = T // G
    C = HC + 1
    n = f"m{layer}_"
    (sh, hn, hf, nh, nl, gl, uf, uh, ul, xb, st, mean, rs, tmp, dev), _ = mem.place(
        K.mlp_end, mem.end, (n + "shifted", [P, 2, G, P], F32), (n + "hn", [P, G, D], F32),
        (n + "hnT", [P, KC, GT], F32), (n + "hnT_hi", [P, 2, KC, GT], F32R), (n + "hnT_lo", [P, 2, KC, GT], F32R),
        (n + "gelu", [P, 2, GT], F32), (n + "u", [P, 2, GT], F32), (n + "u_hi", [P, 2, GT], F32R),
        (n + "u_lo", [P, 2, GT], F32R), (n + "xb", [P, G, D], F32), (n + "stats", [P, G, 12], F32),
        (n + "mean", [P, G], F32), (n + "rstd", [P, G], F32), (n + "tmp", [P, G], F32), (n + "dev", [P, G, 4], F32))

    def schedule(eng, group, rebase=None):
        with eng.Fori(0, NG // 2) as p:
            for r in range(2):
                rebase and rebase(2 * p + r)
                group(2 * p + r, r)

    def rest(c):
        return slice(0, P) if c < HC else slice(0, HR)

    with nc.Block() as block:

        @block.sync
        def _(sp):
            if not last_layer:
                for dst, src in K.local_loads(layer + 1):
                    sp.dma_start(dst, src).then_inc(K.local_in.sem, 16)

            sp.dma_start(sh[:, 0], A.scratch[0:GT, :].rearrange("(j p) c -> p j c", p=P)).then_inc(s.sh_in[0].sem, 16)
            with sp.Fori(0, NG // 2) as p:
                for r in range(2):
                    g = 2 * p + r
                    sp.wait_ge(*s.normed.room(g + 1, 2))
                    sp.dma_start(sh[:, 1 - r], A.scratch[bass.ds((g + 1) % NG * GT, GT), :]
                                 .rearrange("(j p) c -> p j c", p=P)).then_inc(s.sh_in[1 - r].sem, 16)
            if last_layer:
                out = A.out.rearrange("b (j p) c -> p (b j) c", p=P)
                with sp.Fori(0, NG // 2) as p:
                    for r in range(2):
                        sp.wait_ge(*s.y_done.after(G * (2 * p + r) + G))
                        sp.dma_start(out[:, bass.ds(G * (2 * p + r), G), :], X[:, bass.ds(G * (2 * p + r), G), :]
                                     ).then_inc(s.stored[r].sem, 16)
                for r in range(2):
                    sp.wait_ge(*s.stored[r].after(16 * (NG // 2)))
            for r in range(2):
                sp.wait_ge(*s.sh_in[r].after(16 * (NG // 2 + 1 - r)))
            if not last_layer:
                sp.wait_ge(*K.local_in.after(16 * len(K.local_loads(layer)) * (layer + 2)))

        @block.gpsimd
        def _(pool):
            with pool.Fori(0, NG) as g:
                tiles = bass.ds(G * g, G)
                pool.wait_ge(*s.y_done.room(G * g + G - 1, G))
                nc.gpsimd.tensor_tensor(xb[:], X[:, tiles], K.b2[:, layer].unsqueeze(1).to_broadcast([P, G, D]),
                                        ALU.add).then_inc(s.based.sem, 1)
                if last_layer:
                    pool.wait_ge(*s.based.after(2 * g + 1))
                    nc.gpsimd.tensor_tensor(xb[:], xb[:], K.H[:, tiles], ALU.add).then_inc(s.based.sem, 1)

        @block.scalar
        def _(act):
            for h, raw in ((w1h, w1raw), (w2h, w2raw)):
                nc.scalar.activation(h[:], raw[:], ACT.Copy).then_inc(s.w_hi.sem, 1)

            def hidden_hi(c, at):
                act.wait_ge(*s.u.after(at + 1))
                act.wait_ge(*s.w2_done.room(at, 2))
                nc.scalar.activation(uh[rest(c), c % 2], uf[rest(c), c % 2], ACT.Copy).then_inc(s.u_hi.sem, 1)

            def normed_hi(r, count):
                for c in range(KC):
                    act.wait_ge(*s.hf.after(KC * count + c + 1))
                    nc.scalar.activation(nh[:, r, c], hf[:, c], ACT.Copy).then_inc(s.n_hi.sem, 1)

            def group(g, r):
                for c in range(C):
                    bank = 2 * (c % 2)
                    act.wait_ge(*s.ag_full.after(C * g + c + 1))
                    act.wait_ge(*s.u.room(C * g + c, 2))
                    if c < HC:
                        nc.scalar.activation(gl[:, c % 2], ps[:, bank + 1], ACT.Gelu,
                                             bias=K.b1[:, layer, HC + c:HC + c + 1]).then_inc(s.gelu.sem, 1)
                    else:
                        nc.scalar.activation(gl[0:HR, c % 2], ps[GR:GR + HR, bank], ACT.Gelu,
                                             bias=K.b1[GR:GR + HR, layer, 2 * HC:2 * HC + 1]).then_inc(s.gelu.sem, 1)
                    hidden_hi(c, C * g + c)
                    if c == 4:
                        normed_hi(1 - r, g + 1)

            normed_hi(0, 0)
            schedule(act, group)

        @block.vector
        def _(dve):
            chain = Chain(dve, s.dve.sem)
            for k, (lo, raw, hi) in enumerate(((w1l, w1raw, w1h), (w2l, w2raw, w2h))):
                dve.wait_ge(*s.w_hi.after(k + 1))
                nc.vector.tensor_tensor(lo[:], raw[:], f32(hi[:]), ALU.subtract).then_inc(s.w_lo.sem, 1)
            norm = Stats(st[:], G, 4, mean[:], rs[:], tmp[:], dev[:])

            def stats(g, r):
                if isinstance(g, int):
                    dve.wait_ge(*s.sh_in[r].after(16 * (g // 2 + 1)))
                else:
                    dve.wait_ge(*s.sh_in[r].after(16 * (g // 2) + 16))
                first = G * (g % NG)
                if r == 0:
                    chain(nc.vector.memset(sh[0:1, r, 0], 0.0))
                for j in range(G):
                    nc.vector.bn_stats(st[:, j, 0:6], X[:, bass.ds(first + j, 1), 0:P])
                    last = nc.vector.bn_stats(st[:, j, 6:12], sh[:, r, j])
                chain(last)

            def normalise(g, r):
                norm.finish(nc, chain)
                first = G * (g % NG)
                for j in range(G):
                    nc.vector.tensor_scalar(hn[:, j:j + 1, 0:P], X[:, bass.ds(first + j, 1), 0:P], mean[:, j:j + 1],
                                            rs[:, j:j + 1], ALU.subtract, ALU.mult)
                    last = nc.vector.tensor_scalar(hn[:, j, P:D], sh[:, r, j], mean[:, j:j + 1], rs[:, j:j + 1],
                                                   ALU.subtract, ALU.mult)
                last.then_inc(s.normed.sem, 1)

            def scaled(count):
                for c in range(KC):
                    dve.wait_ge(*s.n_t.after(KC * count + c + 1))
                    nc.vector.tensor_scalar(hf[:, c], ps[:, 6 + c], K.lg[:, layer, c:c + 1], K.lb[:, layer, c:c + 1],
                                            ALU.mult, ALU.add).then_inc(s.hf.sem, 1)

            def normed_lo(r, count):
                for c in range(KC):
                    dve.wait_ge(*s.n_hi.after(KC * count + c + 1))
                    nc.vector.tensor_tensor(nl[:, r, c], hf[:, c], f32(nh[:, r, c]), ALU.subtract).then_inc(s.n_lo.sem, 1)

            def hidden(c, at):
                bank, rows, col = 2 * (c % 2), rest(c), c if c < HC else 2 * HC
                dve.wait_ge(*s.gelu.after(at + 1))
                nc.vector.scalar_tensor_tensor(uf[rows, c % 2], ps[rows, bank], K.b1[rows, layer, col:col + 1],
                                               gl[rows, c % 2], ALU.add, ALU.mult).then_inc(s.u.sem, 1)
                dve.wait_ge(*s.u_hi.after(at + 1))
                nc.vector.tensor_tensor(ul[rows, c % 2], uf[rows, c % 2], f32(uh[rows, c % 2]),
                                        ALU.subtract).then_inc(s.u_lo.sem, 1)

            def residual(g):
                dve.wait_ge(*s.w2_done.after(C * (g + 1)))
                dve.wait_ge(*s.based.after((2 if last_layer else 1) * (g + 1)))
                for j in range(G):
                    nc.vector.tensor_tensor(X[:, bass.ds(G * g + j, 1)], ps[:, 4 + j // 2:5 + j // 2, j % 2 * D:(j % 2 + 1) * D],
                                            xb[:, j:j + 1], ALU.add).then_inc(s.y_done.sem, 1)

            def group(g, r, tail=True):
                for c in range(C):
                    if c == 1 and tail:
                        residual(g - 1)
                    hidden(c, C * g + c)
                    if c == 1:
                        stats(g + 1, 1 - r)
                    if c == 2:
                        normalise(g + 1, 1 - r)
                    if c == 3:
                        scaled(g + 1)
                    if c == 4:
                        normed_lo(1 - r, g + 1)

            stats(0, 0)
            normalise(0, 0)
            scaled(0)
            normed_lo(0, 0)
            start = chain.n
            group(0, 0, False)
            group(1, 1)
            per_pair = chain.n - start
            with dve.Fori(1, NG // 2) as p:
                chain.rebase(start + per_pair * p)
                group(2 * p, 0)
                group(2 * p + 1, 1)
                assert chain.n == per_pair
            residual(NG - 1)

        @block.tensor
        def _(pe):
            def transposes(count):
                pe.wait_ge(*s.normed.after(count + 1))
                pe.wait_ge(*s.hf.after(KC * count))
                for c in range(KC):
                    for j in range(G):
                        last = nc.tensor.transpose(ps[:, 6 + c, j * P:(j + 1) * P], hn[:, j, c * P:(c + 1) * P], K.ident[:])
                    last.then_inc(s.n_t.sem, 1)

            def up(g, r, c):
                pe.wait_ge(*s.u.room(C * g + c, 2))
                F = HC * P
                parts = ((c * P, P, 0), (F + c * P, P, 1)) if c < HC else ((2 * F, W1C - 2 * F, 0),)
                for at, m, half in parts:
                    for k in range(KC):
                        last = matmul3(nc, ps[0:m, 2 * (c % 2) + half], w1h[:, k, at:at + m], w1l[:, k, at:at + m],
                                       nh[:, r, k], nl[:, r, k], k == 0, k == KC - 1)
                last.then_inc(s.ag_full.sem, 1)

            def down(c, at):
                rows = rest(c)
                pe.wait_ge(*s.u_lo.after(at + 1))
                for j in range(G):
                    t = slice(j * P, (j + 1) * P)
                    out = ps[:, 4 + j // 2, j % 2 * D:(j % 2 + 1) * D]
                    last = matmul3(nc, out, uh[rows, c % 2, t], ul[rows, c % 2, t], w2h[rows, c], w2l[rows, c],
                                   c == 0 and j % 2 == 0, c == C - 1)
                last.then_inc(s.w2_done.sem, 1)

            def group(g, r, tail=True):
                pe.wait_ge(*s.n_lo.after(KC * (g + 1)))
                for c in range(C):
                    up(g, r, c)
                    if c:
                        if c == 1 and tail:
                            pe.wait_ge(*s.y_done.after(G * g))
                        down(c - 1, C * g + c - 1)
                    elif tail:
                        down(C - 1, C * g - 1)
                    if c == 3:
                        transposes(g + 1)

            transposes(0)
            pe.wait_ge(*s.w_lo.after(2))
            group(0, 0, False)
            group(1, 1)
            with pe.Fori(1, NG // 2) as p:
                group(2 * p, 0)
                group(2 * p + 1, 1)
            down(C - 1, C * NG - 1)


class TokCounts:

    def __init__(self, count):
        self.ident = count("ident")
        self.tok_ws = count("tok_ws")
        self.tok_wrow = count("tok_wrow")
        self.txt_in = count("txt_in")
        self.attn_w = count("attn_w")
        self.attn_whi = count("attn_whi")
        self.bias_in = count("bias_in")
        self.bias = count("bias")
        self.tok_wraw = count("tok_wraw")
        self.tok_whi = count("tok_whi")
        self.tok_wlo = count("tok_wlo")
        self.tok_wst = count("tok_wst")
        self.tok_xt = count("tok_xt", 8)
        self.tok_hi = count("tok_hi")
        self.tok_lo = count("tok_lo", 4)
        self.tok_mm = count("tok_mm", 2)
        self.tok_h = count("tok_h", 2)
        self.tok_in = [count(f"tok_in{r}") for r in range(NIMG // P)]


class AttentionCounts:

    def __init__(self, count):
        self.consts_in = count("consts_in")
        self.zeroed = count("zeroed")
        self.attn_set = count("attn_set")
        self.attn_wo_hi = count("attn_wo_hi")
        self.attn_wo_lo = count("attn_wo_lo")
        self.attn_dve = count("attn_dve")
        self.attn_xn = count("attn_xn")
        self.attn_t_full = count("attn_t_full")
        self.attn_t_hi = count("attn_t_hi")
        self.attn_t_done = count("attn_t_done", 2)
        self.attn_a_full = count("attn_a_full")
        self.attn_exp = count("attn_exp")
        self.attn_feat = count("attn_feat", 2)
        self.attn_b_full = count("attn_b_full")
        self.attn_b_done = count("attn_b_done", 2)
        self.attn_kv_mm = count("attn_kv_mm", 2)
        self.attn_kv = count("attn_kv")
        self.attn_o_full = count("attn_o_full")
        self.attn_o = count("attn_o", 4)


class LocalCounts:

    def __init__(self, count):
        self.padded = count("padded")
        self.const_in = count("const_in")
        self.y_done = count("y_done")
        self.turned = count("turned")
        self.qk_t = count("qk_t", 1)
        self.summed = count("summed")
        self.rnorm = count("rnorm")
        self.rotated = count("rotated")
        self.set = count("set")
        self.w_hi = count("w_hi")
        self.x_t = count("x_t")
        self.x_hi = count("x_hi")
        self.negmax = count("negmax")
        self.exped = count("exped")
        self.p_t = count("p_t")
        self.p_done = count("p_done")
        self.o_t = count("o_t")
        self.o_hi = count("o_hi")
        self.qk_full = count("qk_full")
        self.squared = count("squared")
        self.v_full = count("v_full")
        self.o_full = count("o_full")
        self.v_done = count("v_done")
        self.qk_done = count("qk_done")
        self.dve = count("dve")
        self.x_copied = count("x_copied")
        self.w_lo = count("w_lo")
        self.x_done = count("x_done")
        self.scored = count("scored")
        self.masked = count("masked")
        self.o_done = count("o_done")
        self.y_full = count("y_full")
        self.o_norm = count("o_norm")
        self.stored = [count(f"stored{r}") for r in range(2)]


class MlpCounts:

    def __init__(self, count):
        self.normed = count("normed", 1)
        self.y_done = count("y_done", 4)
        self.based = count("based")
        self.w_hi = count("w_hi")
        self.u = count("u", 2)
        self.w2_done = count("w2_done", 2)
        self.u_hi = count("u_hi")
        self.hf = count("hf")
        self.n_hi = count("n_hi")
        self.ag_full = count("ag_full")
        self.gelu = count("gelu")
        self.dve = count("dve")
        self.w_lo = count("w_lo")
        self.n_t = count("n_t")
        self.n_lo = count("n_lo")
        self.u_lo = count("u_lo")
        self.sh_in = [count(f"sh_in{r}") for r in range(2)]
        self.stored = [count(f"stored{r}") for r in range(2)]


class Kept:
    pass


class Arrays:

    def __init__(self, aps, out, scratch):
        self.out, self.scratch = out, scratch
        self.attn_Wg = aps["attn_Wg"]
        self.attn_Wk = aps["attn_Wk"]
        self.attn_Wo = aps["attn_Wo"]
        self.attn_Wq = aps["attn_Wq"]
        self.attn_Wv = aps["attn_Wv"]
        self.attn_bg = aps["attn_bg"]
        self.ffn_b1 = aps["ffn_b1"]
        self.ffn_b2 = aps["ffn_b2"]
        self.ffn_k_scale = aps["ffn_k_scale"]
        self.ffn_ln_b = aps["ffn_ln_b"]
        self.ffn_ln_g = aps["ffn_ln_g"]
        self.ffn_q_scale = aps["ffn_q_scale"]
        self.ffn_w1 = aps["ffn_w1"]
        self.ffn_w2 = aps["ffn_w2"]
        self.ffn_wo = aps["ffn_wo"]
        self.ffn_wqkv = aps["ffn_wqkv"]
        self.flags = aps["flags"]
        self.ident = aps["ident"]
        self.mask_cur = aps["mask_cur"]
        self.mask_prev = aps["mask_prev"]
        self.negs = aps["negs"]
        self.rope_cos = aps["rope_cos"]
        self.rope_sin = aps["rope_sin"]
        self.tok_w = aps["tok_w"]
        self.tok_ws = aps["tok_ws"]
        self.txt = aps["txt"]
        self.x = aps["x"]


def build(nc, names, aps, out, debug=""):
    mem = Memory(nc)
    ctx = ExitStack()
    with ctx:
        credited = []

        def count(name, credit=0):
            c = Count(ctx.enter_context(nc.semaphore("s_" + name)), credit)
            if credit:
                credited.append(c)
            return c

        K = Kept()
        tok_s, attention_s = TokCounts(count), AttentionCounts(count)
        local_s = [LocalCounts(lambda name, credit=0: count(f"l{layer}_{name}", credit)) for layer in range(2)]
        mlp_s = [MlpCounts(lambda name, credit=0: count(f"m{layer}_{name}", credit)) for layer in range(2)]
        A = Arrays(dict(zip(names, aps)), out,
                   nc.dram_tensor("shifted", [N * B + 1, P], F32, kind="Internal").ap())
        K.ps = ctx.enter_context(nc.psum_tensor("ps", [P, 8, 512], F32))
        (K.H, K.X), _ = mem.place(mem.h, mem.const, ("h", [P, T, D], F32), ("x", [P, T, D], F32))
        (K.ident, K.b1, K.b2, K.lg, K.lb, K.zrow, K.attn_bgrows), _ = mem.place(
            mem.const, mem.wb, ("ident", [P, P], F32),
            ("ffn_b1", [P, 2, 2 * HC + 1], F32), ("ffn_b2", [P, 2, D], F32), ("ffn_ln_g", [P, 2, KC], F32),
            ("ffn_ln_b", [P, 2, KC], F32), ("zero_row", [1, P], F32),
            ("attn_bgrows", [3, INNER], BF16))
        (K.attn_wh, K.attn_wl, K.attn_woh, K.attn_wol), _ = mem.place(
            mem.wa, mem.tail, ("attn_w_hi", [P, 4, KC, INNER], F32R), ("attn_w_lo", [P, 4, KC, INNER], F32R),
            ("attn_wo_hi", [P, PAIRS, D], F32R), ("attn_wo_lo", [P, PAIRS, D], F32R))
        (K.attn_wraw,), at = mem.place(mem.wa + 4 * KC * INNER * 4, mem.tail, ("attn_w_raw", [P, 4, KC, INNER], F32))
        (K.attn_woraw,), _ = mem.place(at + PAIRS * D * 4, mem.tail, ("attn_wo_raw", [P, PAIRS, D], F32))
        K.attn_raw = [(K.attn_wraw[:, n], w.rearrange("(c p) n -> p c n", p=P))
                      for n, w in enumerate((A.attn_Wq, A.attn_Wk, A.attn_Wv, A.attn_Wg))]
        K.attn_raw.append((K.attn_woraw[:], A.attn_Wo.rearrange("(m p) n -> p m n", p=P)))
        K.attn_bias = (A.attn_bg.rearrange("(a n) -> a n", a=1).to_broadcast([3, INNER]))
        F = HC * P
        K.ffn_consts = [(K.b2[:], A.ffn_b2.rearrange("(a l) n -> a l n", a=1).to_broadcast([P, 2, D]))]
        for layer in range(2):
            b1 = A.ffn_b1[layer:layer + 1]
            K.ffn_consts += [
                (K.b1[:, layer, 0:HC], b1[:, 0:F].rearrange("a (c p) -> p (a c)", p=P)),
                (K.b1[:, layer, HC:2 * HC], b1[:, HID:HID + F].rearrange("a (c p) -> p (a c)", p=P)),
                (K.b1[0:HR, layer, 2 * HC:2 * HC + 1], b1[:, F:HID].rearrange("a p -> p a")),
                (K.b1[GR:GR + HR, layer, 2 * HC:2 * HC + 1], b1[:, HID + F:2 * HID].rearrange("a p -> p a")),
                (K.lg[:, layer], A.ffn_ln_g[layer:layer + 1].rearrange("a (c p) -> p (a c)", p=P)),
                (K.lb[:, layer], A.ffn_ln_b[layer:layer + 1].rearrange("a (c p) -> p (a c)", p=P))]
        (K.qkv_h, K.qkv_l, K.wo_h, K.wo_l), _ = mem.place(
            mem.wb, mem.wa, ("qkv_hi", [P, KC, 3 * LINNER], F32R), ("qkv_lo", [P, KC, 3 * LINNER], F32R),
            ("wo_hi", [P, LPAIRS, D], F32R), ("wo_lo", [P, LPAIRS, D], F32R))
        (K.qkv_raw,), at = mem.place(mem.wb + KC * 3 * LINNER * 4, mem.wa, ("qkv_raw", [P, KC, 3 * LINNER], F32))
        (K.wo_raw,), _ = mem.place(at + LPAIRS * D * 4, mem.wa, ("wo_raw", [P, LPAIRS, D], F32))
        (K.w1_h, K.w1_l, K.w2_h, K.w2_l), K.mlp_end = mem.place(
            mem.wa, mem.tail, ("w1_hi", [P, KC, W1C], F32R), ("w1_lo", [P, KC, W1C], F32R),
            ("w2_hi", [P, HC + 1, D], F32R), ("w2_lo", [P, HC + 1, D], F32R))
        w1_bytes, w2_bytes = (KC * W1C * 4 + 31) // 32 * 32, (HC + 1) * D * 4
        (K.w1_raw,), at = mem.place(mem.wa + w1_bytes, mem.tail, ("w1_raw", [P, KC, W1C], F32))
        (K.w2_raw,), _ = mem.place(at + w2_bytes, mem.tail, ("w2_raw", [P, HC + 1, D], F32))

        def local_loads(layer):
            return [(K.qkv_raw[:, c], A.ffn_wqkv[layer, c * P:(c + 1) * P, :]) for c in range(KC)] + [
                (K.wo_raw[:], A.ffn_wo[layer].rearrange("(m p) n -> p m n", p=P))]

        def mlp_loads(layer):
            w1 = A.ffn_w1[layer].rearrange("(c p) n -> p c n", p=P)
            F = HC * P
            return [(K.w1_raw[:, :, 0:F], w1[:, :, 0:F]), (K.w1_raw[:, :, F:2 * F], w1[:, :, HID:HID + F]),
                    (K.w1_raw[:, :, 2 * F:2 * F + HR], w1[:, :, F:HID]),
                    (K.w1_raw[:, :, 2 * F + GR:W1C], w1[:, :, HID + F:2 * HID]),
                    (K.w2_raw[:, 0:HC, :], A.ffn_w2[layer, 0:F].rearrange("(c p) n -> p c n", p=P)),
                    (K.w2_raw[0:HR, HC, :], A.ffn_w2[layer, F:HID])]

        K.local_loads, K.mlp_loads = local_loads, mlp_loads
        K.local_in, K.mlp_in = count("local_in"), count("mlp_in")
        with nc.Block() as block:

            @block.gpsimd
            def _(pool):
                for c in credited:
                    pool.sem_inc(c.sem, c.credit)

        tok_phase(nc, tok_s, mem, K, A)
        if debug != 'tok':
            attention_phase(nc, attention_s, mem, K, A)
        if debug not in ('tok', 'attn'):
            for layer in range(1 if debug in ('loc0', 'mlp0') else 2):
                local_phase(nc, local_s[layer], mem, K, A, layer)
                if debug == 'loc0':
                    break
                mlp_phase(nc, mlp_s[layer], mem, K, A, layer, layer == 1)
        if debug == "":
            return
        res = K.H if debug in ('tok', 'attn') else K.X
        with nc.Block() as block:

            @block.sync
            def _(sp):
                with nc.semaphore("s_out") as so:
                    sp.dma_start(out.rearrange("b (j p) c -> p (b j) c", p=P), res[:]).then_inc(so, 16)
                    sp.wait_ge(so, 16)


def arrays(inputs):
    import numpy as np
    out = {name.replace("L0_", ""): np.ascontiguousarray(a) for name, a in inputs.items()}
    out["tok_w"] = out.pop("tok_weight")
    out["tok_ws"] = out.pop("tok_weighted_sum")
    out["ident"] = np.eye(P, dtype=np.float32)
    half = np.arange(0, DH, 2, dtype=np.float32)
    t = np.arange(N, dtype=np.float32)
    freqs = t[:, None] * (1.0 / ROPE_BASE ** (half / DH)).astype(np.float32)[None, :]
    base = (half + 0.4 * DH) / (1.4 * DH)
    scale = base[None, :].astype(np.float32) ** ((t - N // 2) / (WINDOW // 2))[:, None].astype(np.float32)
    c, sn = np.cos(freqs), np.sin(freqs)
    both = lambda a, b: np.concatenate([a, b], 1)
    cos = np.stack([both(c * scale, c * scale), both(c / scale, c / scale)], 1)
    sin = np.stack([both(-sn * scale, sn * scale), both(-sn / scale, sn / scale)], 1)
    for name, table in (("rope_cos", cos), ("rope_sin", sin)):
        out[name] = np.ascontiguousarray(table.reshape(TB, P, 2, DH).transpose(1, 0, 2, 3).astype(np.float32))
    i, j = np.arange(P)[:, None], np.arange(P)[None, :]
    out["mask_prev"] = np.where(i > j, MASKED, 0.0).astype(np.float32)
    out["mask_cur"] = np.where(i < j, MASKED, 0.0).astype(np.float32)
    first = np.arange(T // 2) % (TB // 2) == 0
    out["flags"] = np.tile(np.where(first, 0.0, 1.0).astype(np.float32), (P, 1))
    out["negs"] = np.tile(np.where(first, MASKED, 0.0).astype(np.float32), (P, 1))
    return out


def kernel(**inputs):
    import numpy as np
    import concourse.bacc as bacc
    from concourse.bass_utils import run_bass_kernel_spmd

    nc = bacc.Bacc("TRN2", target_bir_lowering=False, num_devices=1)
    feeds = arrays(inputs)
    aps = [nc.dram_tensor(name, a.shape, mybir.dt.from_np(a.dtype), kind="ExternalInput").ap()
           for name, a in feeds.items()]
    out = nc.dram_tensor("out", (B, N, D), F32, kind="ExternalOutput").ap()
    build(nc, list(feeds), aps, out)
    result = run_bass_kernel_spmd(nc, [feeds], core_ids=[0])
    return np.asarray(result.results[0]["out"])
```

```python
import concourse.bass as bass
from concourse import mybir
from contextlib import ExitStack

F32 = mybir.dt.float32
F32R = mybir.dt.float32r
BF16 = mybir.dt.bfloat16
I32 = mybir.dt.int32
ALU = mybir.AluOpType
ACT = mybir.ActivationFunctionType
AX = mybir.AxisListType

P = 128
B, N, D = 4, 1024, 256
NIMG = 512
DP = 4
TB = N // P
T = B * TB
KC = D // P
HEADS, DH = 16, 64
INNER = HEADS * DH
PAIRS = HEADS // 2
LH = 8
LINNER = LH * DH
LPAIRS = LH // 2
HID = 682
HC = HID // P
HR = HID - HC * P
GR = 64
W1C = 2 * HC * P + GR + HR
SPLITS = T // 2 - 1
FW = -(-(KC * W1C + (HC + 1) * D) // SPLITS) * SPLITS
LN_EPS = 1e-5
MASKED = -1.0e37
LOWEST = -3.0e38
RSQRT_SEED = float(0x5F3759DF)
ROPE_BASE = 10000.0
WINDOW = 128


class Memory:

    def __init__(self, nc):
        self.nc = nc
        base = (nc.sbuf_base + 63) // 64 * 64
        self.h = base
        self.x = self.h + T * D * 4
        self.const = self.x + T * D * 4
        self.wb = self.const + 6080
        self.wa = self.wb + 32768
        self.tail = self.wa + 81920
        self.end = nc.sbuf_usable_end

    def place(self, at, end, *wanted):
        out = []
        for name, shape, dt in wanted:
            size = 2 if dt == BF16 else 4
            for n in shape[1:]:
                size *= n
            out.append(self.nc.alloc_sbuf_tensor_at(name, shape, dt, offset=at))
            at += (size + 31) // 32 * 32
            assert at <= end, (name, at, end)
        return out, at


def f32(ap):
    return ap.bitcast(F32)


class Count:

    def __init__(self, sem, credit):
        self.sem, self.credit = sem, credit

    def after(self, n):
        return self.sem, self.credit + n

    def room(self, n, slots):
        return self.sem, self.credit + n + 1 - slots


class Chain:

    def __init__(self, eng, sem):
        self.eng, self.sem, self.base, self.n = eng, sem, 0, 0

    def __call__(self, ins):
        self.n += 1
        ins.then_inc(self.sem, 1)
        self.eng.wait_ge(self.sem, self.base + self.n)

    def rebase(self, base):
        self.base, self.n = base, 0


def matmul3(nc, out, wh, wl, mh, ml, start, stop):
    nc.tensor.matmul(out, wh, mh, start=start, stop=False, skip_group_check=True)
    nc.tensor.matmul(out, wh, ml, start=False, stop=False, skip_group_check=True)
    return nc.tensor.matmul(out, wl, mh, start=False, stop=stop, skip_group_check=True)


def rsqrt(nc, chain, out, tmp, val, steps=3):
    chain(nc.vector.tensor_scalar(out.bitcast(I32), val.bitcast(I32), -0.5, RSQRT_SEED, ALU.mult, ALU.add))
    for _ in range(steps):
        newton(nc, chain, out, tmp, val)


def newton(nc, chain, out, tmp, val):
    chain(nc.vector.tensor_tensor(tmp, out, out, ALU.mult))
    chain(nc.vector.scalar_tensor_tensor(tmp, tmp, -0.5, val, ALU.mult, ALU.mult))
    chain(nc.vector.scalar_tensor_tensor(out, tmp, 1.5, out, ALU.add, ALU.mult))


class Stats:

    def __init__(self, st, n, groups, mean, rstd, tmp, dev):
        self.st, self.n, self.groups, self.mean, self.rstd, self.tmp, self.dev = st, n, groups, mean, rstd, tmp, dev

    def finish(self, nc, chain):
        self.variance(nc, chain)
        self.deviation(nc, chain)

    def variance(self, nc, chain):
        n, g = self.n, self.groups
        v = self.st.rearrange("p n (g k) -> p n g k", k=3)
        mean, rstd, tmp, dev = self.mean, self.rstd, self.tmp, self.dev
        chain(nc.vector.tensor_reduce(rstd, v[:, :, :, 1], AX.X, ALU.add))
        chain(nc.vector.tensor_scalar(mean, rstd, 1.0 / g, None, ALU.mult))
        chain(nc.vector.tensor_tensor(dev, v[:, :, :, 1], mean.unsqueeze(2).to_broadcast([P, n, g]), ALU.subtract))
        chain(nc.vector.tensor_tensor(dev, dev, dev, ALU.mult))
        chain(nc.vector.tensor_reduce(tmp, dev, AX.X, ALU.add))
        chain(nc.vector.tensor_reduce(rstd, v[:, :, :, 2], AX.X, ALU.add))
        chain(nc.vector.tensor_scalar(rstd, rstd, 1.0 / D, LN_EPS, ALU.mult, ALU.add))
        chain(nc.vector.scalar_tensor_tensor(dev[:, :, 0], tmp, 1.0 / g, rstd, ALU.mult, ALU.add))

    def deviation(self, nc, chain):
        rsqrt(nc, chain, self.rstd, self.tmp, self.dev[:, :, 0])


STATS_STEPS = 8 + 10


def tok_phase(nc, s, mem, K, A):
    ps = K.ps
    NC = DP * KC
    JT = NIMG // P
    (xin, xth, xtl), _ = mem.place(mem.x, mem.const,
                                   ("tok_x", [P, JT, D * DP], F32),
                                   ("tok_xT_hi", [P, 2, NC, P], F32R),
                                   ("tok_xT_lo", [P, 2, NC, P], F32R))
    (wh, wl, ws, wrow), _ = mem.place(mem.tail, mem.end,
                                      ("tok_w_hi", [P, NC, D], F32R), ("tok_w_lo", [P, NC, D], F32R),
                                      ("tok_ws", [P, KC, D], F32), ("tok_wrow", [P, D * DP], F32))
    (wraw, bgrest, bgpart), _ = mem.place(mem.wb, mem.wa, ("tok_w_raw", [P, NC, D], F32),
                                          ("tok_bias_rest", [3, INNER], F32), ("tok_bias_part", [3, INNER], BF16))
    assert B == 4 and JT >= KC, "one of the four weight matrices of the attention is split a batch"
    x_t = A.x.rearrange("b (j p) i d -> b j p (i d)", p=P)
    with nc.Block() as block:

        @block.sync
        def _(sp):
            sp.dma_start(K.ident[:], A.ident).then_inc(s.ident.sem, 16)
            sp.dma_start(ws[:], A.tok_ws.rearrange("(c p) i -> p c i", p=P)).then_inc(s.tok_ws.sem, 16)
            sp.dma_start(wrow[:], A.tok_w.rearrange("(a o) d -> a (o d)", a=1).to_broadcast([P, D * DP])
                         ).then_inc(s.tok_wrow.sem, 16)
            with sp.Fori(0, B) as b:
                for j in range(JT):
                    sp.wait_ge(*s.tok_xt.room(2 * (JT * b + j) + 1, 2 * JT))
                    sp.dma_start(xin[:, j:j + 1, :], x_t[bass.ds(b, 1), j].rearrange("b p c -> p b c")
                                 ).then_inc(s.tok_in[j].sem, 16)
                sp.dma_start(K.H[:, bass.ds(TB * b + JT, TB - JT), :], A.txt.rearrange("b (j p) c -> p (b j) c", p=P)
                             [:, bass.ds((TB - JT) * b, TB - JT), :]).then_inc(s.txt_in.sem, 16)
            sp.wait_ge(*s.txt_in.after(16 * B))

        @block.scalar
        def _(act):
            act.dma_start(bgrest[:], K.attn_bias).then_inc(s.bias_in.sem, 16)
            for raw, src in K.attn_raw:
                act.dma_start(raw, src).then_inc(s.attn_w.sem, 16)
            for d in range(DP):
                act.wait_ge(*s.tok_wraw.after(d + 1))
                w = slice(d * KC, (d + 1) * KC)
                nc.scalar.activation(wh[:, w], wraw[:, w], ACT.Copy).then_inc(s.tok_whi.sem, 1)

            def take(b, j):
                act.wait_ge(*s.tok_mm.after(JT * b + j + 1))
                nc.scalar.activation(K.H[:, bass.ds(TB * b + j, 1), :], ps[:, 4 + j % 2:5 + j % 2, 0:D],
                                     ACT.Copy).then_inc(s.tok_h.sem, 1)

            with act.Fori(0, B) as b:
                for j in range(JT):
                    act.wait_ge(*s.tok_mm.room(JT * b + j, 2))
                    for half in range(2):
                        act.wait_ge(*s.tok_xt.after(2 * (JT * b + j) + half + 1))
                        nc.scalar.activation(xth[:, j % 2, 4 * half:4 * half + 4, :].rearrange("p c t -> p (c t)"),
                                             ps[:, 2 * (j % 2) + half, :], ACT.Copy).then_inc(s.tok_hi.sem, 1)
                    if j:
                        take(b, j - 1)
                    if j >= JT - KC:
                        c = j - (JT - KC)
                        act.wait_ge(*s.attn_w.after(16 * len(K.attn_raw)))
                        nc.scalar.activation(K.attn_wh[:, bass.ds(b, 1), c], K.attn_wraw[:, bass.ds(b, 1), c],
                                             ACT.Copy).then_inc(s.attn_whi.sem, 1)
                take(b, JT - 1)

        @block.vector
        def _(dve):
            chain = Chain(dve, s.bias.sem)
            rest, part, rows = bgrest, bgpart, K.attn_bgrows
            dve.wait_ge(*s.bias_in.after(16))
            dve.wait_ge(*s.ident.after(16))

            def bias_row(k):
                chain(nc.vector.tensor_copy(part[:], rest[:]))
                if k == 0:
                    chain(nc.vector.tensor_scalar(rows[:], part[:], K.ident[0:3, 0:1], None, ALU.mult))
                else:
                    chain(nc.vector.scalar_tensor_tensor(rows[:], part[:], K.ident[0:3, k:k + 1], rows[:],
                                                         ALU.mult, ALU.add))
                if k < 2:
                    chain(nc.vector.tensor_tensor(rest[:], rest[:], part[:], ALU.subtract))

            bias_row(0)
            bias_row(1)
            dve.wait_ge(*s.tok_wrow.after(16))
            dve.wait_ge(*s.tok_wst.after(1))
            wr = wrow[:].rearrange("p (o d) -> p o d", d=DP)
            for d in range(DP):
                for c in range(KC):
                    last = nc.vector.tensor_tensor(wraw[:, d * KC + c, :], ps[:, 6, c * D:(c + 1) * D],
                                                   wr[:, :, d], ALU.mult)
                last.then_inc(s.tok_wraw.sem, 1)
            bias_row(2)
            for d in range(DP):
                dve.wait_ge(*s.tok_whi.after(d + 1))
                w = slice(d * KC, (d + 1) * KC)
                nc.vector.tensor_tensor(wl[:, w], wraw[:, w], f32(wh[:, w]), ALU.subtract).then_inc(s.tok_wlo.sem, 1)
            with dve.Fori(0, B) as b:
                for j in range(JT):
                    for half in range(2):
                        dve.wait_ge(*s.tok_hi.after(2 * (JT * b + j) + half + 1))
                        nc.vector.tensor_tensor(
                            xtl[:, j % 2, 4 * half:4 * half + 4, :].rearrange("p c t -> p (c t)"),
                            ps[:, 2 * (j % 2) + half, :],
                            f32(xth[:, j % 2, 4 * half:4 * half + 4, :].rearrange("p c t -> p (c t)")),
                            ALU.subtract).then_inc(s.tok_lo.sem, 1)
                    if j >= JT - KC:
                        c = j - (JT - KC)
                        dve.wait_ge(*s.attn_whi.after(KC * b + c + 1))
                        w = bass.ds(b, 1)
                        nc.vector.tensor_tensor(K.attn_wl[:, w, c], K.attn_wraw[:, w, c], f32(K.attn_wh[:, w, c]),
                                                ALU.subtract)

        @block.tensor
        def _(pe):
            pe.wait_ge(*s.ident.after(16))
            pe.wait_ge(*s.tok_ws.after(16))
            for c in range(KC):
                for o in range(KC):
                    last = nc.tensor.transpose(ps[:, 6, c * D + o * P:c * D + (o + 1) * P],
                                               ws[:, o, c * P:(c + 1) * P], K.ident[:])
            last.then_inc(s.tok_wst.sem, 1)

            def transposes(b, j):
                pe.wait_ge(*s.tok_in[j].after(16 * b + 16))
                xv = xin[:, j, :].rearrange("p (c i d) -> p d c i", c=KC, d=DP)
                for half in range(2):
                    pe.wait_ge(*s.tok_lo.room(2 * (JT * b + j) + half, 4))
                    for k in range(4):
                        d, c = (4 * half + k) // KC, k % KC
                        last = nc.tensor.transpose(ps[:, 2 * (j % 2) + half, k * P:(k + 1) * P],
                                                   xv[:, d, c, :], K.ident[:])
                    last.then_inc(s.tok_xt.sem, 1)

            def products(b, j):
                pe.wait_ge(*s.tok_wlo.after(DP))
                pe.wait_ge(*s.tok_lo.after(2 * (JT * b + j) + 2))
                pe.wait_ge(*s.tok_h.room(JT * b + j, 2))
                for k in range(NC):
                    last = matmul3(nc, ps[:, 4 + j % 2, 0:D], xth[:, j % 2, k, :], xtl[:, j % 2, k, :],
                                   wh[:, k, :], wl[:, k, :], k == 0, k == NC - 1)
                last.then_inc(s.tok_mm.sem, 1)

            with pe.Fori(0, B) as b:
                for j in range(JT):
                    transposes(b, j)
                    if j:
                        products(b, j - 1)
                products(b, JT - 1)


def attention_phase(nc, s, mem, K, A):
    ps = K.ps
    H = K.H
    wh, wl = K.attn_wh, K.attn_wl
    woh, wol, woraw = K.attn_woh, K.attn_wol, K.attn_woraw
    Q, KEY, VAL, GATE = range(4)
    VC = P + 1
    OC = P + 2
    GROUPS = ((0, 3), (3, 6), (6, 8))
    HALF = INNER // 2
    (xth, xtl, th, og), _ = mem.place(
        mem.x, mem.const, ("attn_xT_hi", [P, KC, N], F32R), ("attn_xT_lo", [P, KC, N], F32R),
        ("attn_tanh", [P, 2, INNER], F32), ("attn_out", [P, 2, INNER], F32))
    (ks, vs, kv, oth, otl), _ = mem.place(
        mem.wb, mem.wa, ("attn_k", [P, 2, INNER], F32), ("attn_v", [P, 2, PAIRS, VC], F32),
        ("attn_kv", [P, PAIRS, OC], F32), ("attn_oT_hi", [P, PAIRS, P], F32R),
        ("attn_oT_lo", [P, PAIRS, P], F32R))
    (qt, ex, xn, o1, ones, mean, rs, tmp, dev, st, z, zd), _ = mem.place(
        mem.tail, mem.end, ("attn_qT", [P, PAIRS, 2 * P], F32), ("attn_exp", [P, 2, 512], F32),
        ("attn_xn", [P, 2, D], F32), ("attn_o1", [P, 2, 384], F32),
        ("attn_ones", [3, P], BF16), ("attn_mean", [P, TB], F32), ("attn_rstd", [P, TB], F32),
        ("attn_tmp", [P, TB], F32), ("attn_dev", [P, TB, 2], F32), ("attn_stats", [P, TB, 6], F32),
        ("attn_z", [P, 6], F32), ("attn_den", [P, 6], F32))
    bgrows = K.attn_bgrows
    AB, OB, TF, TH = 32, 24, 32, 24

    def t_fill(b, u, k):
        return 8 + TF * b + 8 * (u - 1) + k

    def t_hi(b, u, k):
        return 8 + TH * b + 6 * (u - 1) + k

    with nc.Block() as block:

        @block.sync
        def _(sp):
            for dst, src in K.ffn_consts:
                sp.dma_start(dst, src, allow_slow_non_contiguous=True).then_inc(s.consts_in.sem, 16)
            sp.wait_ge(*s.zeroed.after(1))
            sp.dma_start(A.scratch[0:1, :], K.zrow[:]).then_inc(s.consts_in.sem, 16)
            sp.wait_ge(*s.consts_in.after(16 * (len(K.ffn_consts) + 1)))

        @block.gpsimd
        def _(pool):
            nc.gpsimd.memset(K.zrow[:], 0.0).then_inc(s.zeroed.sem, 1)
            nc.gpsimd.memset(ones[:], 1.0)
            nc.gpsimd.memset(vs[:, :, :, P:VC], 1.0)
            nc.gpsimd.memset(kv[:], 0.0).then_inc(s.attn_set.sem, 1)
            pool.wait_ge(*s.attn_wo_hi.after(1))
            nc.gpsimd.tensor_tensor(wol[:], woraw[:], f32(woh[:]), ALU.subtract).then_inc(s.attn_wo_lo.sem, 1)

        @block.scalar
        def _(act):
            nc.scalar.activation(woh[:], woraw[:], ACT.Copy).then_inc(s.attn_wo_hi.sem, 1)

            def xt_hi(t_bank, tile, hi_n, full_n):
                act.wait_ge(*s.attn_t_full.after(full_n + 1))
                nc.scalar.activation(xth[:, :, tile * P:(tile + 1) * P],
                                     ps[:, t_bank, 0:D].rearrange("p (c t) -> p c t", c=KC),
                                     ACT.Copy).then_inc(s.attn_t_hi.sem, 1)

            for j in range(TB):
                xt_hi(6 + j % 2, j, j, j)

            def exp_(n, at):
                act.wait_ge(*s.attn_a_full.after(n + 1))
                act.wait_ge(*s.attn_feat.room(n, 2))
                nc.scalar.activation(ex[:, at % 2], ps[:, at % 2], ACT.Exp).then_inc(s.attn_exp.sem, 1)

            def tanh_(b, n):
                act.wait_ge(*s.attn_o.after(OB * b + 3 * (n - 1)))
                for half in range(2):
                    act.wait_ge(*s.attn_b_full.after(AB * b + 16 + 2 * n + half + 1))
                    nc.scalar.activation(th[:, n % 2, half * HALF:(half + 1) * HALF], ps[:, 2 + half],
                                         ACT.Tanh, scale=0.5).then_inc(s.attn_b_done.sem, 1)

            def ot_hi(b, u, which):
                act.wait_ge(*s.attn_t_full.after(t_fill(b, u, 2) if which else t_fill(b, u, -3)))
                for half in range(2):
                    k = 3 * which + half
                    act.wait_ge(*s.attn_t_full.after(t_fill(b, u, k) + 1))
                    nc.scalar.activation(oth[:, 4 * half:4 * half + 4, :].rearrange("p c t -> p (c t)"),
                                         ps[:, 6 + k % 2], ACT.Copy).then_inc(s.attn_t_hi.sem, 1)

            def value(b, j, half):
                act.wait_ge(*s.attn_kv_mm.room(TB * b + j, 2))
                act.wait_ge(*s.attn_b_full.after(AB * b + 2 * j + half + 1))
                nc.scalar.activation(vs[:, j % 2, 4 * half:4 * half + 4, 0:P],
                                     ps[:, 2 + half].rearrange("p (m c) -> p m c", m=4),
                                     ACT.Copy).then_inc(s.attn_b_done.sem, 1)

            for half in range(2):
                exp_(half, half)
            for half in range(2):
                value(0, 0, half)
            with act.Fori(0, B) as b:
                for j in range(1, TB):
                    for half in range(2):
                        exp_(AB * b + 2 * j + half, half)
                    for half in range(2):
                        value(b, j, half)
                for u in range(TB // 2):
                    for f in range(2):
                        exp_(AB * b + 16 + 4 * u + f, f)
                    if u:
                        ot_hi(b, u, 0)
                    for f in range(2, 4):
                        exp_(AB * b + 16 + 4 * u + f, f)
                    tanh_(b, 2 * u)
                    if u:
                        ot_hi(b, u, 1)
                    tanh_(b, 2 * u + 1)
                    if u:
                        for w in range(2):
                            xt_hi(6 + w, 2 * u - 2 + w, t_hi(b, u, 4 + w), t_fill(b, u, 6 + w))
                u = TB // 2
                ot_hi(b, u, 0)
                for half in range(2):
                    exp_(AB * (b + 1) + half, half)
                value(b + 1, 0, 0)
                ot_hi(b, u, 1)
                value(b + 1, 0, 1)
                for w in range(2):
                    xt_hi(6 + w, 2 * u - 2 + w, t_hi(b, u, 4 + w), t_fill(b, u, 6 + w))

        @block.vector
        def _(dve):
            chain = Chain(dve, s.attn_dve.sem)

            def stats(tile, j):
                return nc.vector.bn_stats(st[:, j, :], H[:, tile, :])

            norm = Stats(st[:], TB, 2, mean[:], rs[:], tmp[:], dev[:])

            def normalise(tile, j):
                nc.vector.tensor_scalar(xn[:, j % 2], H[:, tile, :], mean[:, j:j + 1], rs[:, j:j + 1],
                                        ALU.subtract, ALU.mult).then_inc(s.attn_xn.sem, 1)

            def xt_lo(t_bank, tile, hi_n):
                dve.wait_ge(*s.attn_t_hi.after(hi_n + 1))
                cols = slice(tile * P, (tile + 1) * P)
                nc.vector.tensor_tensor(xtl[:, :, cols], ps[:, t_bank, 0:D].rearrange("p (c t) -> p c t", c=KC),
                                        f32(xth[:, :, cols]), ALU.subtract).then_inc(s.attn_t_done.sem, 1)

            for j in range(TB):
                last = stats(j, j)
            chain(last)
            norm.finish(nc, chain)
            for j in range(TB):
                if j >= 2:
                    dve.wait_ge(*s.attn_t_full.after(j - 1))
                normalise(j, j)
                if j:
                    xt_lo(6 + (j - 1) % 2, j - 1, j - 1)
            xt_lo(6 + (TB - 1) % 2, TB - 1, TB - 1)

            def feature(n, at, dst):
                dve.wait_ge(*s.attn_exp.after(n + 1))
                chain(nc.vector.tensor_scalar(ex[:, at % 2], ex[:, at % 2], 1.0, None, ALU.min))
                src, e = ps[:, at % 2], ex[:, at % 2]
                if len(dst.shape) == 3:
                    src, e = (v.rearrange("p (m t) -> p m t", m=2) for v in (src, e))
                nc.vector.scalar_tensor_tensor(dst, src, 0.0, e, ALU.max, ALU.add).then_inc(s.attn_feat.sem, 1)

            def ot_lo(b, u, which):
                for half in range(2):
                    dve.wait_ge(*s.attn_t_hi.after(t_hi(b, u, 2 * which + half) + 1))
                    m = slice(4 * half, 4 * half + 4)
                    nc.vector.tensor_tensor(otl[:, m, :].rearrange("p c t -> p (c t)"), ps[:, 6 + (3 * which + half) % 2],
                                            f32(oth[:, m, :].rearrange("p c t -> p (c t)")),
                                            ALU.subtract).then_inc(s.attn_t_done.sem, 1)

            def residual(b, u, which):
                dve.wait_ge(*s.attn_t_full.after(t_fill(b, u, 3 * which + 2) + 1))
                tile = H[:, bass.ds(TB * b + 2 * u - 2 + which, 1), :]
                nc.vector.tensor_tensor(tile, ps[:, 6 + which % 2:7 + which % 2, 0:D], tile,
                                        ALU.add).then_inc(s.attn_t_done.sem, 1)

            def gated(b, n, *groups):
                for g in groups:
                    m0, m1 = GROUPS[g]
                    w = m1 - m0
                    dve.wait_ge(*s.attn_o_full.after(OB * b + 3 * n + g + 1))
                    out = ps[:, 4 + (3 * n + g) % 2, 0:w * OC].rearrange("p (m c) -> p m c", c=OC)
                    chain(nc.vector.tensor_scalar(zd[:, 0:2 * w].rearrange("p (m e) -> p m e", e=2), out[:, :, P:OC],
                                                  1e-6, 2.0 * DH ** 0.5, ALU.max, ALU.mult))
                    chain(nc.vector.reciprocal(z[:, 0:2 * w], zd[:, 0:2 * w]))
                    zb = z[:, 0:2 * w].rearrange("p (m e) -> p m e", e=2).unsqueeze(3).to_broadcast([P, w, 2, DH])
                    chain(nc.vector.tensor_tensor(o1[:, g % 2, 0:w * P].rearrange("p (m e d) -> p m e d", e=2, d=DH),
                                                  out[:, :, 0:P].rearrange("p m (e d) -> p m e d", e=2), zb, ALU.mult))
                    if g == 0:
                        dve.wait_ge(*s.attn_b_done.after(AB * b + 16 + 2 * n + 2))
                    nc.vector.scalar_tensor_tensor(og[:, n % 2, m0 * P:m1 * P], th[:, n % 2, m0 * P:m1 * P], 1.0,
                                                   o1[:, g % 2, 0:w * P], ALU.add, ALU.mult).then_inc(s.attn_o.sem, 1)

            PER_BATCH = 2 * TB + 4 * (TB // 2) + 1 + STATS_STEPS + 3 * len(GROUPS) * TB
            def key_features(b, j):
                for half in range(2):
                    feature(AB * b + 2 * j + half, half, ks[:, j % 2, half * HALF:(half + 1) * HALF])

            key_features(0, 0)
            start = chain.n
            dve.wait_ge(*s.attn_set.after(1))
            with dve.Fori(0, B) as b:
                chain.rebase(start + PER_BATCH * b)
                dve.wait_ge(*s.attn_t_done.after(t_fill(b, 1, 0)))
                nxt = TB * ((b + 1) % B)
                for j in range(TB):
                    if j:
                        key_features(b, j)
                    last = stats(bass.ds(nxt + j, 1), j)
                chain(last)
                norm.finish(nc, chain)
                dve.wait_ge(*s.attn_kv_mm.after(TB * b + TB))
                for g, (m0, m1) in enumerate(GROUPS):
                    acc = ps[:, 4 + g, 0:(m1 - m0) * VC].rearrange("p (m c) -> p m c", c=VC)
                    for e in range(2):
                        r = slice(e * DH, (e + 1) * DH)
                        nc.vector.tensor_copy(kv[r, m0:m1, e * DH:(e + 1) * DH], acc[r, :, e * DH:(e + 1) * DH])
                        last = nc.vector.tensor_copy(kv[r, m0:m1, P + e:P + e + 1], acc[r, :, P:VC])
                last.then_inc(s.attn_kv.sem, 1)
                for u in range(TB // 2 + 1):
                    if u == TB // 2:
                        ot_lo(b, u, 0)
                    if u < TB // 2:
                        for f in range(2):
                            feature(AB * b + 16 + 4 * u + f, f, qt[:, 2 * f:2 * f + 2, :])
                    if u:
                        for w in range(2):
                            normalise(bass.ds(nxt + 2 * u - 2 + w, 1), 2 * u - 2 + w)
                    if u == TB // 2:
                        key_features(b + 1, 0)
                    if 0 < u < TB // 2:
                        ot_lo(b, u, 0)
                    if u < TB // 2:
                        for f in range(2, 4):
                            feature(AB * b + 16 + 4 * u + f, f, qt[:, 2 * f:2 * f + 2, :])
                    if u:
                        residual(b, u, 0)
                        ot_lo(b, u, 1)
                    if u < TB // 2:
                        gated(b, 2 * u, 0, 1, 2)
                        gated(b, 2 * u + 1, 0)
                    if u:
                        residual(b, u, 1)
                    if u < TB // 2:
                        gated(b, 2 * u + 1, 1)
                    if u:
                        for w in range(2):
                            xt_lo(6 + w, 2 * u - 2 + w, t_hi(b, u, 4 + w))
                        dve.wait_ge(*s.attn_t_done.after(t_fill(b, u, 5) + 1))
                        for w in range(2):
                            tile = bass.ds(TB * b + 2 * u - 2 + w, 1)
                            nc.vector.bn_stats(K.h_stats[:, tile], H[:, tile])
                    if u < TB // 2:
                        gated(b, 2 * u + 1, 2)
                assert chain.n == PER_BATCH, (chain.n, PER_BATCH)

        @block.tensor
        def _(pe):
            def xt(bank, xn_n, slot, fill_n):
                pe.wait_ge(*s.attn_xn.after(xn_n + 1))
                pe.wait_ge(*s.attn_t_done.room(fill_n, 2))
                for c in range(KC):
                    last = nc.tensor.transpose(ps[:, bank, c * P:(c + 1) * P], xn[:, slot, c * P:(c + 1) * P], K.ident[:])
                last.then_inc(s.attn_t_full.sem, 1)

            def rows(w, tile, bank0, full, free, count, bias, halves=(0, 1)):
                for half in halves:
                    cols = slice(half * HALF, (half + 1) * HALF)
                    out = ps[:, bank0 + half]
                    pe.wait_ge(*free.room(count + half, 2))
                    if bias:
                        nc.tensor.matmul(out, ones[:], bgrows[:, cols], start=True, stop=False, skip_group_check=True)
                    for c in range(KC):
                        t = slice(tile * P, (tile + 1) * P)
                        last = matmul3(nc, out, xth[:, c, t], xtl[:, c, t], wh[:, w, c, cols], wl[:, w, c, cols],
                                       c == 0 and not bias, c == KC - 1)
                    last.then_inc(full.sem, 1)

            def kv_products(b, j):
                pe.wait_ge(*s.attn_feat.after(AB * b + 2 * j + 2))
                pe.wait_ge(*s.attn_b_done.after(AB * b + 2 * j + 2))
                for g, (m0, m1) in enumerate(GROUPS):
                    for m in range(m0, m1):
                        last = nc.tensor.matmul(ps[:, 4 + g, (m - m0) * VC:(m - m0 + 1) * VC],
                                                ks[:, j % 2, m * P:(m + 1) * P], vs[:, j % 2, m, :],
                                                start=(j == 0 and m == m0), stop=(j == TB - 1),
                                                skip_group_check=True)
                last.then_inc(s.attn_kv_mm.sem, 1)

            def queries(b, u, f):
                n = AB * b + 16 + 4 * u + f
                pe.wait_ge(*s.attn_feat.room(n, 2))
                for i in range(2):
                    m = 2 * f + i
                    for c in range(KC):
                        t = slice(2 * u * P, (2 * u + 2) * P)
                        last = matmul3(nc, ps[:, f % 2, i * 2 * P:(i + 1) * 2 * P], wh[:, Q, c, m * P:(m + 1) * P],
                                       wl[:, Q, c, m * P:(m + 1) * P], xth[:, c, t], xtl[:, c, t],
                                       c == 0, c == KC - 1)
                last.then_inc(s.attn_a_full.sem, 1)

            def outputs(b, u, which, *groups):
                n = 2 * u + which
                pe.wait_ge(*s.attn_feat.after(AB * b + 16 + 4 * u + 4))
                pe.wait_ge(*s.attn_kv.after(b + 1))
                for g in groups:
                    m0, m1 = GROUPS[g]
                    pe.wait_ge(*s.attn_o.room(OB * b + 3 * n + g, 2))
                    for m in range(m0, m1):
                        last = nc.tensor.matmul(ps[:, 4 + (3 * n + g) % 2, (m - m0) * OC:(m - m0 + 1) * OC],
                                                qt[:, m, which * P:(which + 1) * P], kv[:, m, :],
                                                start=True, stop=True)
                    last.then_inc(s.attn_o_full.sem, 1)

            def out_transposes(b, u, which):
                n = 2 * (u - 1) + which
                pe.wait_ge(*s.attn_o.after(OB * b + 3 * n + 3))
                for half in range(2):
                    k = 3 * which + half
                    pe.wait_ge(*s.attn_t_done.room(t_fill(b, u, k), 2))
                    for i in range(4):
                        m = 4 * half + i
                        last = nc.tensor.transpose(ps[:, 6 + k % 2, i * P:(i + 1) * P],
                                                   og[:, which, m * P:(m + 1) * P], K.ident[:])
                    last.then_inc(s.attn_t_full.sem, 1)

            def out_products(b, u, which):
                k = 3 * which + 2
                pe.wait_ge(*s.attn_t_done.after(t_fill(b, u, k)))
                for m in range(PAIRS):
                    last = matmul3(nc, ps[:, 6 + k % 2, 0:D], oth[:, m, :], otl[:, m, :], woh[:, m, :], wol[:, m, :],
                                   m == 0, m == PAIRS - 1)
                last.then_inc(s.attn_t_full.sem, 1)

            def keys(b, j):
                rows(KEY, j, 0, s.attn_a_full, s.attn_feat, AB * b + 2 * j, False)

            def values(b, j, halves=(0, 1)):
                rows(VAL, j, 2, s.attn_b_full, s.attn_b_done, AB * b + 2 * j, False, halves)

            pe.wait_ge(*s.attn_set.after(1))
            for j in range(TB):
                xt(6 + j % 2, j, j % 2, j)
                if j == 1:
                    pe.wait_ge(*s.attn_t_done.after(1))
                    keys(0, 0)
                if j == 3:
                    values(0, 0)
            with pe.Fori(0, B) as b:
                for j in range(TB):
                    if j < TB - 1:
                        keys(b, j + 1)
                        values(b, j + 1)
                    if j == 0:
                        pe.wait_ge(*s.attn_t_done.after(t_fill(b, 1, 0)))
                        pe.wait_ge(*s.attn_o.after(OB * b))
                    kv_products(b, j)
                pe.wait_ge(*s.attn_wo_lo.after(1))
                for u in range(TB // 2 + 1):
                    if u < TB // 2:
                        queries(b, u, 0)
                        queries(b, u, 1)
                    if u:
                        out_transposes(b, u, 0)
                    if u < TB // 2:
                        queries(b, u, 2)
                        queries(b, u, 3)
                    else:
                        keys(b + 1, 0)
                    if u:
                        out_products(b, u, 0)
                    if u == TB // 2:
                        values(b + 1, 0, (0,))
                    if u < TB // 2:
                        count = AB * b + 16 + 4 * u
                        rows(GATE, 2 * u, 2, s.attn_b_full, s.attn_b_done, count, True)
                    if u:
                        out_transposes(b, u, 1)
                    if u == TB // 2:
                        values(b + 1, 0, (1,))
                    if u < TB // 2:
                        outputs(b, u, 0, 0, 1)
                        rows(GATE, 2 * u + 1, 2, s.attn_b_full, s.attn_b_done, count + 2, True, (0,))
                        outputs(b, u, 0, 2)
                        rows(GATE, 2 * u + 1, 2, s.attn_b_full, s.attn_b_done, count + 2, True, (1,))
                        outputs(b, u, 1, 0)
                    if u:
                        out_products(b, u, 1)
                    if u < TB // 2:
                        outputs(b, u, 1, 1)
                    if u:
                        for w in range(2):
                            xt(6 + w, TB * (b + 1) + 2 * u - 2 + w, w, t_fill(b, u, 6 + w))
                    if u < TB // 2:
                        outputs(b, u, 1, 2)


def wait(eng, count, n):
    if not isinstance(n, int) or n > 0:
        eng.wait_ge(*count.after(n))


def local_phase(nc, s, mem, K, A, layer):
    ps, X = K.ps, K.X
    wh, wl, woh, wol = K.qkv_h, K.qkv_l, K.wo_h, K.wo_l
    LW = KC * 3 * LINNER + LPAIRS * D
    PIECES = [slice(i, i + LW // 4) for i in range(0, LW, LW // 4)]
    XW = P + 2
    (idle, xc, xt, sq, t1, t2, rot, qt, kt, vv, pm, pt, osb, oth, otl, cos, sin, mask_e, mask_o, prev, flags, negs, qks,
     ss, rn, tmp, mx, nb, rsum, rinv, mean, rs, tmp32, dev), _ = mem.place(
        K.mlp_end, mem.end,
        (f"l{layer}_idle", [P, 1], F32), (f"l{layer}_x", [P, 2, D], F32),
        (f"l{layer}_xT", [P, 2, 2, 2 * XW], F32R), (f"l{layer}_sq", [P, 2, LINNER], F32),
        (f"l{layer}_t1", [P, 2, LINNER], F32), (f"l{layer}_t2", [P, 2, LINNER], F32),
        (f"l{layer}_rot", [P, 2, LINNER], F32), (f"l{layer}_qT", [P, LPAIRS, P], F32),
        (f"l{layer}_kT", [P, 2, LPAIRS, P], F32), (f"l{layer}_v", [P, 2, LINNER], F32),
        (f"l{layer}_probs", [P, LPAIRS, 4 * P], F32), (f"l{layer}_probsT", [P, 2, 4 * P], F32),
        (f"l{layer}_o", [P, LINNER], F32), (f"l{layer}_oT_hi", [P, LINNER], F32R),
        (f"l{layer}_oT_lo", [P, LINNER], F32R), (f"l{layer}_cos", [P, TB, 2, DH], F32),
        (f"l{layer}_sin", [P, TB, 2, DH], F32), (f"l{layer}_mask_even", [P, 2 * P], F32),
        (f"l{layer}_mask_odd", [P, 2 * P], F32), (f"l{layer}_mask_prev", [P, P], F32),
        (f"l{layer}_flags", [P, T // 2], F32), (f"l{layer}_negs", [P, T // 2], F32),
        (f"l{layer}_qkscale", [P, 2, DH], F32), (f"l{layer}_ss", [P, 2 * LH], F32),
        (f"l{layer}_rnorm", [P, 2 * LH], F32), (f"l{layer}_tmp", [P, 2 * LH], F32),
        (f"l{layer}_max", [P, LH], F32), (f"l{layer}_negmax", [P, LH], F32), (f"l{layer}_rowsum", [P, LH], F32),
        (f"l{layer}_rowinv", [P, LH], F32), (f"l{layer}_mean", [P, T], F32),
        (f"l{layer}_rstd", [P, T], F32),
        (f"l{layer}_tmp32", [P, T], F32), (f"l{layer}_dev", [P, T, 2], F32))

    def schedule(eng, step, rebase=None, piece=None):
        for n in (0, 1):
            rebase and rebase(None)
            step(n, n, True, n >= 1, False)
        with eng.Fori(1, T // 2) as p:
            rebase and rebase(p - 1)
            piece and piece(p - 1)
            for r in range(2):
                step(2 * p + r, r, True, True, True)
        rebase and rebase(T // 2 - 1)
        step(T, 0, False, True, True)
        step(T + 1, 1, False, False, True)

    def turn(r, k):
        return 5 + (r + k) % 2

    OT, Y, XT = 2, 5, 6
    PT = (3, 4, 0, 1)

    with nc.Block() as block:

        @block.sync
        def _(sp):
            sp.dma_start(flags[:], A.flags).then_inc(s.flags_in.sem, 16)
            if layer == 0:
                for dst, src in K.local_loads(layer):
                    sp.dma_start(dst, src).then_inc(K.local_in.sem, 16)
            for dst, src in ((cos[:], A.rope_cos), (sin[:], A.rope_sin), (prev[:], A.mask_prev),
                             (mask_o[:, P:2 * P], A.mask_cur), (mask_e[:, 0:P], A.mask_cur),
                             (mask_o[:, 0:P], A.mask_prev), (negs[:], A.negs),
                             (qks[:, 0, :], A.ffn_q_scale[layer:layer + 1].to_broadcast([P, DH])),
                             (qks[:, 1, :], A.ffn_k_scale[layer:layer + 1].to_broadcast([P, DH]))):
                sp.dma_start(dst, src).then_inc(s.const_in.sem, 16)
            sp.wait_ge(*s.padded.after(1))
            for dst, src in K.mlp_loads(layer):
                sp.dma_start(dst, src).then_inc(K.mlp_in.sem, 16)
            with sp.Fori(0, T // 2) as p:
                for r in range(2):
                    sp.wait_ge(*s.y_done.after(2 * p + r + 1))
                    sp.wait_ge(*K.rows_stored[r].after(16 * (layer * T // 2 + p)))
                    sp.dma_start(A.scratch[bass.ds((2 * p + r) * P + 1, P), :].rearrange("(o p) c -> p o c", o=1),
                                 X[:, bass.ds(2 * p + r, 1), P:D]).then_inc(K.rows_stored[r].sem, 16)
            sp.wait_ge(*K.mlp_in.after(16 * len(K.mlp_loads(layer)) * (layer + 1)))

        @block.gpsimd
        def _(pool):
            nc.gpsimd.memset(K.w1_raw[:, :, 2 * HC * P + HR:2 * HC * P + GR], 0.0)
            nc.gpsimd.memset(K.w_raw[:, KC * W1C + HC * D:FW], 0.0).then_inc(s.padded.sem, 1)
            nc.gpsimd.memset(kt[:, 1], 0.0)
            nc.gpsimd.memset(vv[:, 1], 0.0)
            nc.gpsimd.memset(xt[:, 1].bitcast(F32), 0.0).then_inc(s.set.sem, 1)

            def window(t):
                pool.wait_ge(*s.turned.after(t + 1))
                pool.wait_ge(*s.qk_t.after(2 * t))
                nc.gpsimd.tensor_tensor(rot[:], t1[:], t2[:], ALU.add).then_inc(s.summed.sem, 1)
                pool.wait_ge(*s.summed.after(t + 1))
                pool.wait_ge(*s.rnorm.after(t + 1))
                r = rot[:].rearrange("p a (h d) -> p (a h) d", d=DH)
                nc.gpsimd.tensor_tensor(r, r, rn[:].unsqueeze(2).to_broadcast([P, 2 * LH, DH]),
                                        ALU.mult).then_inc(s.rotated.sem, 1)

            with pool.Fori(0, 2) as t:
                window(t)
            with pool.Fori(1, T // 2) as p:
                window(2 * p)
                pool.wait_ge(*s.ffn_hi.after(p))
                piece = bass.ds((FW // SPLITS) * (p - 1), FW // SPLITS)
                nc.gpsimd.tensor_tensor(K.w_l[:, piece], K.w_raw[:, piece], f32(K.w_h[:, piece]), ALU.subtract)
                window(2 * p + 1)

        @block.scalar
        def _(act):
            if layer == 0:
                act.wait_ge(*K.local_in.after(16 * len(K.local_loads(layer))))
                for piece in PIECES:
                    nc.scalar.activation(K.local_h[:, piece], K.local_raw[:, piece], ACT.Copy).then_inc(s.w_hi.sem, 1)

            def x_hi(t, r, bank):
                wait(act, s.x_t, t + 1)
                nc.scalar.activation(xt[:, r, 0, :].rearrange("p (c w) -> p c w", w=XW)[:, :, 0:P],
                                     ps[:, bank, 0:D].rearrange("p (c w) -> p c w", c=KC),
                                     ACT.Copy).then_inc(s.x_hi.sem, 1)

            def exps(t, pair):
                wait(act, s.negmax, 2 * t + pair // 2 + 1)
                for e in range(2):
                    h = 2 * pair + e
                    v = pm[:, pair, e * 2 * P:(e + 1) * 2 * P]
                    last = nc.scalar.activation(v, v, ACT.Exp, bias=nb[:, h:h + 1], scale=8.0,
                                                accum_out=rsum[:, h:h + 1])
                last.then_inc(s.exped.sem, 1)

            def probs_out(t, pair, r):
                wait(act, s.p_t, 4 * t + pair + 1)
                nc.scalar.activation(pt[:, pair % 2], ps[:, turn(r, PT[pair])], ACT.Copy).then_inc(s.p_done.sem, 1)

            def step(n, r, a, b, c):
                if a:
                    wait(act, s.qk_full, n + 1)
                    wait(act, s.rnorm, n)
                    nc.scalar.activation(sq[:], ps[:, 0:2], ACT.Square).then_inc(s.squared.sem, 1)
                if c:
                    probs_out(n - 2, 2, r)
                    probs_out(n - 2, 3, r)
                if b:
                    for k, dst in enumerate((qt[:], kt[:, 1 - r])):
                        wait(act, s.qk_t, 2 * (n - 1) + k + 1)
                        nc.scalar.activation(dst.rearrange("p m t -> p (m t)"), ps[:, 3 + k],
                                             ACT.Copy).then_inc(s.qk_done.sem, 1)
                if c:
                    wait(act, s.o_t, n - 1)
                    nc.scalar.activation(oth[:], ps[:, turn(r, OT)], ACT.Copy).then_inc(s.o_hi.sem, 1)
                if b:
                    exps(n - 1, 0)
                    exps(n - 1, 1)
                    probs_out(n - 1, 0, r)
                    wait(act, s.v_full, n)
                    wait(act, s.o_full, n - 1)
                    nc.scalar.activation(vv[:, 1 - r], ps[:, 2], ACT.Copy).then_inc(s.v_done.sem, 1)
                    probs_out(n - 1, 1, r)
                if a:
                    x_hi(n + 1, 1 - r, turn(r, XT))
                if b:
                    exps(n - 1, 2)
                    exps(n - 1, 3)

            def ffn_piece(k):
                act.wait_ge(*K.mlp_in.after(16 * len(K.mlp_loads(layer)) * (layer + 1)))
                piece = bass.ds((FW // SPLITS) * k, FW // SPLITS)
                nc.scalar.activation(K.w_h[:, piece], K.w_raw[:, piece], ACT.Copy).then_inc(s.ffn_hi.sem, 1)

            x_hi(0, 0, turn(1, XT))
            schedule(act, step, piece=ffn_piece)

        @block.vector
        def _(dve):
            chain = Chain(dve, s.dve.sem)
            if layer == 0:
                Stats(K.h_stats[:], T, 2, mean[:], rs[:], tmp32[:], dev[:]).finish(nc, chain)
            HF = DH // 2

            def x_lo(t, r, bank):
                wait(dve, s.x_hi, t + 1)
                hi, lo = (xt[:, r, k, :].rearrange("p (c w) -> p c w", w=XW)[:, :, 0:P] for k in (0, 1))
                chain(nc.vector.tensor_tensor(lo, ps[:, bank, 0:D].rearrange("p (c w) -> p c w", c=KC), f32(hi),
                                              ALU.subtract))
                flag = 1.0 if r else flags[:, bass.ds(t // 2 % (T // 2), 1)]
                nc.vector.tensor_scalar(xt[:, r, :, XW - 1:XW], f32(xt[:, 1 - r, :, 2 * XW - 3:2 * XW - 2]), flag, None,
                                        ALU.mult).then_inc(s.x_done.sem, 1)

            def scores(t, half, mask):
                wait(dve, s.scored, 2 * t + half + 1)
                nc.vector.memset(idle[:], 0.0)
                for h in range(4 * half, 4 * half + 4):
                    pair, e, at = h // 2, h % 2, h // 2 % 2 * 2 * P
                    last = nc.vector.tensor_tensor_reduce(
                        pm[:, pair, e * 2 * P:(e + 1) * 2 * P], ps[:, 3 + e, at:at + 2 * P],
                        mask[:], 1.0, LOWEST, ALU.add, ALU.max, mx[:, h:h + 1])
                last.then_inc(s.masked.sem, 1)
                wait(dve, s.masked, 2 * t + half + 1)
                h = slice(4 * half, 4 * half + 4)
                nc.vector.tensor_scalar(nb[:, h], mx[:, h], -8.0, None, ALU.mult).then_inc(s.negmax.sem, 1)

            def normalise(dst, t):
                tile = bass.ds(t, 1)
                return nc.vector.tensor_scalar(dst, K.H[:, tile], mean[:, tile], rs[:, tile], ALU.subtract, ALU.mult)

            def x_copy(t, r):
                tile = bass.ds(t, 1)
                if layer == 0:
                    last = normalise(xc[:, r:r + 1], t)
                else:
                    last = nc.vector.tensor_scalar(xc[:, r:r + 1], X[:, tile], 1.0, None, ALU.mult)
                last.then_inc(s.x_copied.sem, 1)

            def step(n, r, a, b, c):
                if a:
                    x_copy((n + 1) % T, 1 - r)
                    if layer == 0:
                        normalise(X[:, bass.ds(n, 1)], n)
                mask = mask_o if r == 0 else mask_e
                if b and r == 1:
                    chain(nc.vector.tensor_scalar(mask_e[:, P:2 * P], prev[:], negs[:, bass.ds((n - 1) // 2, 1)], None,
                                                  ALU.add))
                if a:
                    wait(dve, s.squared, n + 1)
                    wait(dve, s.summed, n)
                    w = bass.ds(n % TB, 1)
                    q = ps[:, 0:2].rearrange("p a (h d) -> p a h d", d=DH)
                    cw = cos[:, w].rearrange("p o a d -> p a o d").to_broadcast([P, 2, LH, DH])
                    nc.vector.tensor_tensor(t1[:].rearrange("p a (h d) -> p a h d", d=DH), q, cw, ALU.mult)
                    t2v = t2[:].rearrange("p a (h d) -> p a h d", d=DH)
                    for e in range(2):
                        here, there = slice(e * HF, (e + 1) * HF), slice((1 - e) * HF, (2 - e) * HF)
                        sw = sin[:, w, :, here].rearrange("p o a d -> p a o d").to_broadcast([P, 2, LH, HF])
                        last = nc.vector.tensor_tensor(t2v[:, :, :, here], q[:, :, :, there], sw, ALU.mult)
                    last.then_inc(s.turned.sem, 1)
                if c:
                    wait(dve, s.o_full, n - 1)
                    chain(nc.vector.reciprocal(rinv[:], rsum[:]))
                    nc.vector.tensor_tensor(osb[:].rearrange("p (h d) -> p h d", d=DH),
                                            ps[:, 7].rearrange("p (h d) -> p h d", d=DH),
                                            rinv[:].unsqueeze(2).to_broadcast([P, LH, DH]),
                                            ALU.mult).then_inc(s.o_norm.sem, 1)
                if b:
                    scores(n - 1, 0, mask)
                if c:
                    wait(dve, s.o_hi, n - 1)
                    nc.vector.tensor_tensor(otl[:], ps[:, turn(r, OT)], f32(oth[:]), ALU.subtract).then_inc(s.o_done.sem, 1)
                if a:
                    wait(dve, s.rotated, n)
                    chain(nc.vector.tensor_reduce(ss[:], sq[:].rearrange("p a (h d) -> p (a h) d", d=DH), AX.X, ALU.add))
                if b:
                    scores(n - 1, 1, mask)
                if a:
                    chain(nc.vector.tensor_scalar(ss[:], ss[:], 1e-24, None, ALU.max))
                    rsqrt(nc, chain, rn[:], tmp[:], ss[:], 2)
                    x_lo(n + 1, 1 - r, turn(r, XT))
                    newton(nc, chain, rn[:], tmp[:], ss[:])
                    dve.sem_inc(s.rnorm.sem, 1)
                if c:
                    wait(dve, s.y_full, n - 1)
                    tile = X[:, bass.ds(n - 2, 1), :]
                    nc.vector.tensor_tensor(tile, ps[:, turn(r, Y):turn(r, Y) + 1, 0:D], tile,
                                            ALU.add).then_inc(s.y_done.sem, 1)

            x_copy(0, 0)
            if layer == 0:
                for k, piece in enumerate(PIECES):
                    dve.wait_ge(*s.w_hi.after(k + 1))
                    nc.vector.tensor_tensor(K.local_l[:, piece], K.local_raw[:, piece], f32(K.local_h[:, piece]),
                                            ALU.subtract).then_inc(s.w_lo.sem, 1)
            dve.wait_ge(*s.set.after(1))
            dve.wait_ge(*s.flags_in.after(16))
            x_lo(0, 0, turn(1, XT))
            dve.wait_ge(*s.const_in.after(144))
            nc.vector.tensor_tensor(cos[:], cos[:], qks[:].unsqueeze(1).to_broadcast([P, TB, 2, DH]), ALU.mult)
            for e in range(2):
                last = nc.vector.tensor_tensor(sin[:, :, :, e * HF:(e + 1) * HF], sin[:, :, :, e * HF:(e + 1) * HF],
                                               qks[:, :, (1 - e) * HF:(2 - e) * HF].unsqueeze(1)
                                               .to_broadcast([P, TB, 2, HF]), ALU.mult)
            chain(last)
            before = None
            PER_PAIR = 1 + 2 * (12 + 1 + 1)

            def rebase(p):
                nonlocal before
                if p is None:
                    chain.rebase(chain.base + chain.n)
                    return
                if before is None:
                    before = chain.base + chain.n
                else:
                    assert chain.n == PER_PAIR, (chain.n, PER_PAIR)
                chain.rebase(before + PER_PAIR * p)

            schedule(dve, step, rebase)

        @block.tensor
        def _(pe):
            def x_t(t, r, bank):
                wait(pe, s.x_copied, t + 1)
                for c in range(KC):
                    last = nc.tensor.transpose(ps[:, bank, c * P:(c + 1) * P],
                                               xc[:, r, c * P:(c + 1) * P], K.ident[:])
                last.then_inc(s.x_t.sem, 1)

            def project(n, r, w, bank):
                cols = slice(w * LINNER, (w + 1) * LINNER)
                for c in range(KC):
                    at = XW * c - c
                    last = matmul3(nc, ps[:, bank], xt[:, r, 0, at:at + P], xt[:, r, 1, at:at + P],
                                   wh[:, c, cols], wl[:, c, cols], c == 0, c == KC - 1)
                return last

            def score(t, half):
                for pair in (2 * half, 2 * half + 1):
                    for e in range(2):
                        rows, at = slice(e * DH, (e + 1) * DH), pair % 2 * 2 * P
                        last = nc.tensor.matmul(ps[:, 3 + e, at:at + 2 * P], qt[rows, pair, :],
                                                kt[rows, :, pair, :], start=True, stop=True)
                last.then_inc(s.scored.sem, 1)

            def probs_t(t, pair, r):
                wait(pe, s.exped, 4 * t + pair + 1)
                for k in range(4):
                    last = nc.tensor.transpose(ps[:, turn(r, PT[pair]), k * P:(k + 1) * P],
                                               pm[:, pair, k * P:(k + 1) * P], K.ident[:])
                last.then_inc(s.p_t.sem, 1)

            def values(t, pair):
                wait(pe, s.p_done, 4 * t + pair + 1)
                for e in range(2):
                    h = 2 * pair + e
                    for w in range(2):
                        last = nc.tensor.matmul(ps[:, 7, h * DH:(h + 1) * DH],
                                                pt[:, pair % 2, (2 * e + w) * P:(2 * e + w + 1) * P],
                                                vv[:, w, h * DH:(h + 1) * DH], start=(w == 0), stop=(w == 1))
                if pair == LPAIRS - 1:
                    last.then_inc(s.o_full.sem, 1)

            def step(n, r, a, b, c):
                t = n - 1
                if a or b:
                    wait(pe, s.x_done, n + 1)
                if a:
                    wait(pe, s.turned, n)
                    project(n, r, 0, 0)
                    project(n, r, 1, 1).then_inc(s.qk_full.sem, 1)
                if c:
                    wait(pe, s.y_done, n - 2)
                    probs_t(n - 2, 2, r)
                    probs_t(n - 2, 3, r)
                if b:
                    wait(pe, s.rotated, n)
                    wait(pe, s.masked, 2 * t)
                    for k in range(2):
                        for m in range(LPAIRS):
                            last = nc.tensor.transpose(ps[:, 3 + k, m * P:(m + 1) * P], rot[:, k, m * P:(m + 1) * P],
                                                       K.ident[:])
                        last.then_inc(s.qk_t.sem, 1)
                if c:
                    values(n - 2, 2)
                    values(n - 2, 3)
                if b:
                    wait(pe, s.qk_done, 2 * n)
                    score(t, 0)
                if c:
                    wait(pe, s.o_norm, n - 1)
                    for m in range(LPAIRS):
                        last = nc.tensor.transpose(ps[:, turn(r, OT), m * P:(m + 1) * P], osb[:, m * P:(m + 1) * P],
                                                   K.ident[:])
                    last.then_inc(s.o_t.sem, 1)
                if b:
                    wait(pe, s.v_done, t)
                    project(t, 1 - r, 2, 2).then_inc(s.v_full.sem, 1)
                    wait(pe, s.masked, 2 * t + 1)
                    score(t, 1)
                    probs_t(t, 0, r)
                if c:
                    wait(pe, s.o_done, n - 1)
                if b:
                    probs_t(t, 1, r)
                if c:
                    if b:
                        wait(pe, s.p_done, 4 * t + 1)
                    for m in range(LPAIRS):
                        cols = slice(m * P, (m + 1) * P)
                        last = matmul3(nc, ps[:, turn(r, Y), 0:D], oth[:, cols], otl[:, cols], woh[:, m, :], wol[:, m, :],
                                       m == 0, m == LPAIRS - 1)
                    last.then_inc(s.y_full.sem, 1)
                if a:
                    if b:
                        wait(pe, s.p_done, 4 * t + 2)
                    x_t(n + 1, 1 - r, turn(r, XT))
                if b:
                    wait(pe, s.o_norm, t)
                    wait(pe, s.v_done, n)
                    values(t, 0)
                    values(t, 1)

            x_t(0, 0, turn(1, XT))
            if layer == 0:
                pe.wait_ge(*s.w_lo.after(len(PIECES)))
            schedule(pe, step)


def mlp_phase(nc, s, mem, K, A, layer, last_layer):
    ps, X = K.ps, K.X
    w1h, w1l, w2h, w2l = K.w1_h, K.w1_l, K.w2_h, K.w2_l
    G = 4
    GT = G * P
    NG = T // G
    C = HC + 1
    n = f"m{layer}_"
    (sh, hn, hf, nh, nl, gl, uf, uh, ul, xb, st, mean, rs, tmp, dev), _ = mem.place(
        K.mlp_end, mem.end, (n + "shifted", [P, 2, G, P], F32), (n + "hn", [P, G, D], F32),
        (n + "hnT", [P, KC, GT], F32), (n + "hnT_hi", [P, 2, KC, GT], F32R), (n + "hnT_lo", [P, 2, KC, GT], F32R),
        (n + "gelu", [P, 2, GT], F32), (n + "u", [P, 2, GT], F32), (n + "u_hi", [P, 2, GT], F32R),
        (n + "u_lo", [P, 2, GT], F32R), (n + "xb", [P, G, D], F32), (n + "stats", [P, G, 12], F32),
        (n + "mean", [P, G], F32), (n + "rstd", [P, G], F32), (n + "tmp", [P, G], F32), (n + "dev", [P, G, 4], F32))

    def schedule(eng, group, rebase=None):
        with eng.Fori(0, NG // 2) as p:
            for r in range(2):
                rebase and rebase(2 * p + r)
                group(2 * p + r, r)

    def rest(c):
        return slice(0, P) if c < HC else slice(0, HR)

    with nc.Block() as block:

        @block.sync
        def _(sp):
            sp.dma_start(sh[:, 0], A.scratch[0:GT, :].rearrange("(j p) c -> p j c", p=P)).then_inc(s.sh_in[0].sem, 16)
            if not last_layer:
                for dst, src in K.local_loads(layer + 1):
                    sp.dma_start(dst, src).then_inc(K.local_in.sem, 16)
            with sp.Fori(0, NG // 2) as p:
                for r in range(2):
                    g = 2 * p + r
                    sp.wait_ge(*s.normed.room(g + 1, 2))
                    if r == 0:
                        for k in range(2):
                            sp.wait_ge(*K.rows_stored[k].after(16 * (layer + 1) * T // 2))
                    sp.dma_start(sh[:, 1 - r], A.scratch[bass.ds((g + 1) % NG * GT, GT), :]
                                 .rearrange("(j p) c -> p j c", p=P)).then_inc(s.sh_in[1 - r].sem, 16)
            if last_layer:
                out = A.out.rearrange("b (j p) c -> p (b j) c", p=P)
                with sp.Fori(0, NG // 2) as p:
                    for r in range(2):
                        sp.wait_ge(*s.y_done.after(G * (2 * p + r) + G))
                        sp.dma_start(out[:, bass.ds(G * (2 * p + r), G), :], X[:, bass.ds(G * (2 * p + r), G), :]
                                     ).then_inc(s.stored[r].sem, 16)
                for r in range(2):
                    sp.wait_ge(*s.stored[r].after(16 * (NG // 2)))
            for r in range(2):
                sp.wait_ge(*s.sh_in[r].after(16 * (NG // 2 + 1 - r)))
            if not last_layer:
                sp.wait_ge(*K.local_in.after(16 * len(K.local_loads(layer)) * (layer + 2)))

        @block.gpsimd
        def _(pool):
            with pool.Fori(0, NG) as g:
                if not last_layer:
                    pool.wait_ge(*s.local_hi.after(g + 1))
                    piece = bass.ds(K.local_piece * g, K.local_piece)
                    nc.gpsimd.tensor_tensor(K.local_l[:, piece], K.local_raw[:, piece], f32(K.local_h[:, piece]),
                                            ALU.subtract)
                tiles = bass.ds(G * g, G)
                pool.wait_ge(*s.y_done.room(G * g + G - 1, G))
                nc.gpsimd.tensor_tensor(xb[:], X[:, tiles], K.b2[:, layer].unsqueeze(1).to_broadcast([P, G, D]),
                                        ALU.add).then_inc(s.based.sem, 1)
                if last_layer:
                    pool.wait_ge(*s.based.after(2 * g + 1))
                    nc.gpsimd.tensor_tensor(xb[:], xb[:], K.H[:, tiles], ALU.add).then_inc(s.based.sem, 1)

        @block.scalar
        def _(act):
            def hidden_hi(c, at):
                act.wait_ge(*s.u.after(at + 1))
                act.wait_ge(*s.w2_done.room(at, 2))
                nc.scalar.activation(uh[rest(c), c % 2], uf[rest(c), c % 2], ACT.Copy).then_inc(s.u_hi.sem, 1)

            def normed_hi(r, count):
                for c in range(KC):
                    act.wait_ge(*s.hf.after(KC * count + c + 1))
                    nc.scalar.activation(nh[:, r, c], hf[:, c], ACT.Copy).then_inc(s.n_hi.sem, 1)

            def group(g, r):
                for c in range(C):
                    bank = 2 * (c % 2)
                    act.wait_ge(*s.ag_full.after(C * g + c + 1))
                    act.wait_ge(*s.u.room(C * g + c, 2))
                    if c < HC:
                        nc.scalar.activation(gl[:, c % 2], ps[:, bank + 1], ACT.Gelu,
                                             bias=K.b1[:, layer, HC + c:HC + c + 1]).then_inc(s.gelu.sem, 1)
                    else:
                        nc.scalar.activation(gl[0:HR, c % 2], ps[GR:GR + HR, bank], ACT.Gelu,
                                             bias=K.b1[GR:GR + HR, layer, 2 * HC:2 * HC + 1]).then_inc(s.gelu.sem, 1)
                    hidden_hi(c, C * g + c)
                    if c == 2 and not last_layer:
                        act.wait_ge(*K.local_in.after(16 * len(K.local_loads(layer)) * (layer + 2)))
                        piece = bass.ds(K.local_piece * g, K.local_piece)
                        nc.scalar.activation(K.local_h[:, piece], K.local_raw[:, piece],
                                             ACT.Copy).then_inc(s.local_hi.sem, 1)
                    if c == 4:
                        normed_hi(1 - r, g + 1)

            normed_hi(0, 0)
            schedule(act, group)

        @block.vector
        def _(dve):
            chain = Chain(dve, s.dve.sem)
            norm = Stats(st[:], G, 4, mean[:], rs[:], tmp[:], dev[:])

            def stats(g, r):
                first = G * (g % NG)
                for j in range(G):
                    nc.vector.bn_stats(st[:, j, 0:6], X[:, bass.ds(first + j, 1), 0:P])
                dve.wait_ge(*s.sh_in[r].after(16 * (g // 2) + 16))
                if r == 0:
                    chain(nc.vector.memset(sh[0:1, r, 0], 0.0))
                for j in range(G):
                    last = nc.vector.bn_stats(st[:, j, 6:12], sh[:, r, j])
                chain(last)

            def normalise(g, r):
                first = G * (g % NG)
                for j in range(G):
                    nc.vector.tensor_scalar(hn[:, j:j + 1, 0:P], X[:, bass.ds(first + j, 1), 0:P], mean[:, j:j + 1],
                                            rs[:, j:j + 1], ALU.subtract, ALU.mult)
                    last = nc.vector.tensor_scalar(hn[:, j, P:D], sh[:, r, j], mean[:, j:j + 1], rs[:, j:j + 1],
                                                   ALU.subtract, ALU.mult)
                last.then_inc(s.normed.sem, 1)

            def scaled(count):
                for c in range(KC):
                    dve.wait_ge(*s.n_t.after(KC * count + c + 1))
                    nc.vector.tensor_scalar(hf[:, c], ps[:, 6 + c], K.lg[:, layer, c:c + 1], K.lb[:, layer, c:c + 1],
                                            ALU.mult, ALU.add).then_inc(s.hf.sem, 1)

            def normed_lo(r, count):
                for c in range(KC):
                    dve.wait_ge(*s.n_hi.after(KC * count + c + 1))
                    nc.vector.tensor_tensor(nl[:, r, c], hf[:, c], f32(nh[:, r, c]), ALU.subtract).then_inc(s.n_lo.sem, 1)

            def hidden(c, at, between=None):
                bank, rows, col = 2 * (c % 2), rest(c), c if c < HC else 2 * HC
                dve.wait_ge(*s.gelu.after(at + 1))
                nc.vector.scalar_tensor_tensor(uf[rows, c % 2], ps[rows, bank], K.b1[rows, layer, col:col + 1],
                                               gl[rows, c % 2], ALU.add, ALU.mult).then_inc(s.u.sem, 1)
                between and between()
                dve.wait_ge(*s.u_hi.after(at + 1))
                nc.vector.tensor_tensor(ul[rows, c % 2], uf[rows, c % 2], f32(uh[rows, c % 2]),
                                        ALU.subtract).then_inc(s.u_lo.sem, 1)

            def residual(g):
                dve.wait_ge(*s.w2_done.after(C * (g + 1)))
                dve.wait_ge(*s.based.after((2 if last_layer else 1) * (g + 1)))
                for j in range(G):
                    nc.vector.tensor_tensor(X[:, bass.ds(G * g + j, 1)], ps[:, 4 + j // 2:5 + j // 2, j % 2 * D:(j % 2 + 1) * D],
                                            xb[:, j:j + 1], ALU.add).then_inc(s.y_done.sem, 1)

            def group(g, r, tail=True):
                for c in range(C):
                    if c == 5:
                        normed_lo(1 - r, g + 1)
                    between = None
                    if c == 0 and tail:
                        between = lambda: residual(g - 1)
                    if c == 4:
                        between = lambda: scaled(g + 1)
                    hidden(c, C * g + c, between)
                    if c == 0:
                        stats(g + 1, 1 - r)
                    if c == 1:
                        norm.variance(nc, chain)
                    if c == 2:
                        norm.deviation(nc, chain)
                    if c == 3:
                        normalise(g + 1, 1 - r)

            stats(0, 0)
            norm.finish(nc, chain)
            normalise(0, 0)
            scaled(0)
            normed_lo(0, 0)
            start = chain.n
            group(0, 0, False)
            group(1, 1)
            per_pair = chain.n - start
            with dve.Fori(1, NG // 2) as p:
                chain.rebase(start + per_pair * p)
                group(2 * p, 0)
                group(2 * p + 1, 1)
                assert chain.n == per_pair
            residual(NG - 1)

        @block.tensor
        def _(pe):
            def transposes(count):
                pe.wait_ge(*s.normed.after(count + 1))
                pe.wait_ge(*s.hf.after(KC * count))
                for c in range(KC):
                    for j in range(G):
                        last = nc.tensor.transpose(ps[:, 6 + c, j * P:(j + 1) * P], hn[:, j, c * P:(c + 1) * P], K.ident[:])
                    last.then_inc(s.n_t.sem, 1)

            def up(g, r, c):
                pe.wait_ge(*s.u.room(C * g + c, 2))
                F = HC * P
                parts = ((c * P, P, 0), (F + c * P, P, 1)) if c < HC else ((2 * F, W1C - 2 * F, 0),)
                for at, m, half in parts:
                    for k in range(KC):
                        last = matmul3(nc, ps[0:m, 2 * (c % 2) + half], w1h[:, k, at:at + m], w1l[:, k, at:at + m],
                                       nh[:, r, k], nl[:, r, k], k == 0, k == KC - 1)
                last.then_inc(s.ag_full.sem, 1)

            def down(c, at):
                rows = rest(c)
                pe.wait_ge(*s.u_lo.after(at + 1))
                for j in range(G):
                    t = slice(j * P, (j + 1) * P)
                    out = ps[:, 4 + j // 2, j % 2 * D:(j % 2 + 1) * D]
                    last = matmul3(nc, out, uh[rows, c % 2, t], ul[rows, c % 2, t], w2h[rows, c], w2l[rows, c],
                                   c == 0 and j % 2 == 0, c == C - 1)
                last.then_inc(s.w2_done.sem, 1)

            def group(g, r, tail=True):
                pe.wait_ge(*s.n_lo.after(KC * (g + 1)))
                for c in range(C):
                    up(g, r, c)
                    if c:
                        if c == 1 and tail:
                            pe.wait_ge(*s.y_done.after(G * g))
                        down(c - 1, C * g + c - 1)
                    elif tail:
                        down(C - 1, C * g - 1)
                    if c == 4:
                        transposes(g + 1)

            transposes(0)
            group(0, 0, False)
            group(1, 1)
            with pe.Fori(1, NG // 2) as p:
                group(2 * p, 0)
                group(2 * p + 1, 1)
            down(C - 1, C * NG - 1)


class TokCounts:

    def __init__(self, count):
        self.ident = count("ident")
        self.tok_ws = count("tok_ws")
        self.tok_wrow = count("tok_wrow")
        self.txt_in = count("txt_in")
        self.attn_w = count("attn_w")
        self.attn_whi = count("attn_whi")
        self.bias_in = count("bias_in")
        self.bias = count("bias")
        self.tok_wraw = count("tok_wraw")
        self.tok_whi = count("tok_whi")
        self.tok_wlo = count("tok_wlo")
        self.tok_wst = count("tok_wst")
        self.tok_xt = count("tok_xt", 8)
        self.tok_hi = count("tok_hi")
        self.tok_lo = count("tok_lo", 4)
        self.tok_mm = count("tok_mm", 2)
        self.tok_h = count("tok_h", 2)
        self.tok_in = [count(f"tok_in{r}") for r in range(NIMG // P)]


class AttentionCounts:

    def __init__(self, count):
        self.consts_in = count("consts_in")
        self.zeroed = count("zeroed")
        self.attn_set = count("attn_set")
        self.attn_wo_hi = count("attn_wo_hi")
        self.attn_wo_lo = count("attn_wo_lo")
        self.attn_dve = count("attn_dve")
        self.attn_xn = count("attn_xn")
        self.attn_t_full = count("attn_t_full")
        self.attn_t_hi = count("attn_t_hi")
        self.attn_t_done = count("attn_t_done", 2)
        self.attn_a_full = count("attn_a_full")
        self.attn_exp = count("attn_exp")
        self.attn_feat = count("attn_feat", 2)
        self.attn_b_full = count("attn_b_full")
        self.attn_b_done = count("attn_b_done", 2)
        self.attn_kv_mm = count("attn_kv_mm", 2)
        self.attn_kv = count("attn_kv")
        self.attn_o_full = count("attn_o_full")
        self.attn_o = count("attn_o", 4)


class LocalCounts:

    def __init__(self, count):
        self.padded = count("padded")
        self.const_in = count("const_in")
        self.flags_in = count("flags_in")
        self.y_done = count("y_done", 1)
        self.turned = count("turned")
        self.qk_t = count("qk_t", 1)
        self.summed = count("summed")
        self.rnorm = count("rnorm")
        self.rotated = count("rotated")
        self.set = count("set")
        self.ffn_hi = count("ffn_hi")
        self.w_hi = count("w_hi")
        self.x_t = count("x_t")
        self.x_hi = count("x_hi")
        self.negmax = count("negmax")
        self.exped = count("exped")
        self.p_t = count("p_t")
        self.p_done = count("p_done")
        self.o_t = count("o_t")
        self.o_hi = count("o_hi")
        self.qk_full = count("qk_full")
        self.squared = count("squared")
        self.v_full = count("v_full")
        self.o_full = count("o_full")
        self.v_done = count("v_done")
        self.qk_done = count("qk_done")
        self.dve = count("dve")
        self.x_copied = count("x_copied")
        self.w_lo = count("w_lo")
        self.x_done = count("x_done")
        self.scored = count("scored")
        self.masked = count("masked")
        self.o_done = count("o_done")
        self.y_full = count("y_full")
        self.o_norm = count("o_norm")


class MlpCounts:

    def __init__(self, count):
        self.normed = count("normed", 1)
        self.y_done = count("y_done", 4)
        self.based = count("based")
        self.local_hi = count("local_hi")
        self.u = count("u", 2)
        self.w2_done = count("w2_done", 2)
        self.u_hi = count("u_hi")
        self.hf = count("hf")
        self.n_hi = count("n_hi")
        self.ag_full = count("ag_full")
        self.gelu = count("gelu")
        self.dve = count("dve")
        self.n_t = count("n_t")
        self.n_lo = count("n_lo")
        self.u_lo = count("u_lo")
        self.sh_in = [count(f"sh_in{r}") for r in range(2)]
        self.stored = [count(f"stored{r}") for r in range(2)]


class Kept:
    pass


class Arrays:

    def __init__(self, aps, out, scratch):
        self.out, self.scratch = out, scratch
        self.attn_Wg = aps["attn_Wg"]
        self.attn_Wk = aps["attn_Wk"]
        self.attn_Wo = aps["attn_Wo"]
        self.attn_Wq = aps["attn_Wq"]
        self.attn_Wv = aps["attn_Wv"]
        self.attn_bg = aps["attn_bg"]
        self.ffn_b1 = aps["ffn_b1"]
        self.ffn_b2 = aps["ffn_b2"]
        self.ffn_k_scale = aps["ffn_k_scale"]
        self.ffn_ln_b = aps["ffn_ln_b"]
        self.ffn_ln_g = aps["ffn_ln_g"]
        self.ffn_q_scale = aps["ffn_q_scale"]
        self.ffn_w1 = aps["ffn_w1"]
        self.ffn_w2 = aps["ffn_w2"]
        self.ffn_wo = aps["ffn_wo"]
        self.ffn_wqkv = aps["ffn_wqkv"]
        self.flags = aps["flags"]
        self.ident = aps["ident"]
        self.mask_cur = aps["mask_cur"]
        self.mask_prev = aps["mask_prev"]
        self.negs = aps["negs"]
        self.rope_cos = aps["rope_cos"]
        self.rope_sin = aps["rope_sin"]
        self.tok_w = aps["tok_w"]
        self.tok_ws = aps["tok_ws"]
        self.txt = aps["txt"]
        self.x = aps["x"]


def build(nc, names, aps, out):
    mem = Memory(nc)
    ctx = ExitStack()
    with ctx:
        credited = []

        def count(name, credit=0):
            c = Count(ctx.enter_context(nc.semaphore("s_" + name)), credit)
            if credit:
                credited.append(c)
            return c

        K = Kept()
        tok_s, attention_s = TokCounts(count), AttentionCounts(count)
        local_s = [LocalCounts(lambda name, credit=0: count(f"l{layer}_{name}", credit)) for layer in range(2)]
        mlp_s = [MlpCounts(lambda name, credit=0: count(f"m{layer}_{name}", credit)) for layer in range(2)]
        A = Arrays(dict(zip(names, aps)), out,
                   nc.dram_tensor("shifted", [N * B + 1, P], F32, kind="Internal").ap())
        K.ps = ctx.enter_context(nc.psum_tensor("ps", [P, 8, 512], F32))
        (K.H, K.X), _ = mem.place(mem.h, mem.const, ("h", [P, T, D], F32), ("x", [P, T, D], F32))
        (K.ident, K.b1, K.b2, K.lg, K.lb, K.zrow, K.attn_bgrows, K.h_stats), _ = mem.place(
            mem.const, mem.wb, ("ident", [P, P], F32),
            ("ffn_b1", [P, 2, 2 * HC + 1], F32), ("ffn_b2", [P, 2, D], F32), ("ffn_ln_g", [P, 2, KC], F32),
            ("ffn_ln_b", [P, 2, KC], F32), ("zero_row", [1, P], F32),
            ("attn_bgrows", [3, INNER], BF16),
            ("h_stats", [P, T, 6], F32))
        (K.attn_wh, K.attn_wl, K.attn_woh, K.attn_wol), _ = mem.place(
            mem.wa, mem.tail, ("attn_w_hi", [P, 4, KC, INNER], F32R), ("attn_w_lo", [P, 4, KC, INNER], F32R),
            ("attn_wo_hi", [P, PAIRS, D], F32R), ("attn_wo_lo", [P, PAIRS, D], F32R))
        (K.attn_wraw,), at = mem.place(mem.wa + 4 * KC * INNER * 4, mem.tail, ("attn_w_raw", [P, 4, KC, INNER], F32))
        (K.attn_woraw,), _ = mem.place(at + PAIRS * D * 4, mem.tail, ("attn_wo_raw", [P, PAIRS, D], F32))
        K.attn_raw = [(K.attn_wraw[:, n], w.rearrange("(c p) n -> p c n", p=P))
                      for n, w in enumerate((A.attn_Wq, A.attn_Wk, A.attn_Wv, A.attn_Wg))]
        K.attn_raw.append((K.attn_woraw[:], A.attn_Wo.rearrange("(m p) n -> p m n", p=P)))
        K.attn_bias = A.attn_bg.rearrange("(a n) -> a n", a=1).to_broadcast([3, INNER])
        F = HC * P
        K.ffn_consts = [(K.b2[:], A.ffn_b2.rearrange("(a l) n -> a l n", a=1).to_broadcast([P, 2, D]))]
        for layer in range(2):
            b1 = A.ffn_b1[layer:layer + 1]
            K.ffn_consts += [
                (K.b1[:, layer, 0:HC], b1[:, 0:F].rearrange("a (c p) -> p (a c)", p=P)),
                (K.b1[:, layer, HC:2 * HC], b1[:, HID:HID + F].rearrange("a (c p) -> p (a c)", p=P)),
                (K.b1[0:HR, layer, 2 * HC:2 * HC + 1], b1[:, F:HID].rearrange("a p -> p a")),
                (K.b1[GR:GR + HR, layer, 2 * HC:2 * HC + 1], b1[:, HID + F:2 * HID].rearrange("a p -> p a")),
                (K.lg[:, layer], A.ffn_ln_g[layer:layer + 1].rearrange("a (c p) -> p (a c)", p=P)),
                (K.lb[:, layer], A.ffn_ln_b[layer:layer + 1].rearrange("a (c p) -> p (a c)", p=P))]
        QW, LW = KC * 3 * LINNER, KC * 3 * LINNER + LPAIRS * D
        (K.local_h, K.local_l), _ = mem.place(mem.wb, mem.wa, ("local_w_hi", [P, LW], F32R), ("local_w_lo", [P, LW], F32R))
        (K.local_raw,), _ = mem.place(mem.wb + LW * 4, mem.wa, ("local_w_raw", [P, LW], F32))
        K.qkv_h, K.qkv_l, K.qkv_raw = (w[:, 0:QW].rearrange("p (c n) -> p c n", c=KC)
                                       for w in (K.local_h, K.local_l, K.local_raw))
        K.wo_h, K.wo_l, K.wo_raw = (w[:, QW:LW].rearrange("p (m n) -> p m n", n=D)
                                    for w in (K.local_h, K.local_l, K.local_raw))
        K.local_piece = LW // (T // 4)
        (K.w_h, K.w_l), K.mlp_end = mem.place(mem.wa, mem.tail, ("ffn_w_hi", [P, FW], F32R), ("ffn_w_lo", [P, FW], F32R))
        (K.w_raw,), _ = mem.place(mem.wa + FW * 4, mem.tail, ("ffn_w_raw", [P, FW], F32))

        def w1_of(w):
            return w[:, 0:KC * W1C].rearrange("p (c n) -> p c n", c=KC)

        def w2_of(w):
            return w[:, KC * W1C:KC * W1C + (HC + 1) * D].rearrange("p (c n) -> p c n", n=D)

        K.w1_h, K.w1_l, K.w1_raw = w1_of(K.w_h), w1_of(K.w_l), w1_of(K.w_raw)
        K.w2_h, K.w2_l, K.w2_raw = w2_of(K.w_h), w2_of(K.w_l), w2_of(K.w_raw)

        def local_loads(layer):
            return [(K.qkv_raw[:, c], A.ffn_wqkv[layer, c * P:(c + 1) * P, :]) for c in range(KC)] + [
                (K.wo_raw[:], A.ffn_wo[layer].rearrange("(m p) n -> p m n", p=P))]

        def mlp_loads(layer):
            w1 = A.ffn_w1[layer].rearrange("(c p) n -> p c n", p=P)
            F = HC * P
            return [(K.w1_raw[:, :, 0:F], w1[:, :, 0:F]), (K.w1_raw[:, :, F:2 * F], w1[:, :, HID:HID + F]),
                    (K.w1_raw[:, :, 2 * F:2 * F + HR], w1[:, :, F:HID]),
                    (K.w1_raw[:, :, 2 * F + GR:W1C], w1[:, :, HID + F:2 * HID]),
                    (K.w2_raw[:, 0:HC, :], A.ffn_w2[layer, 0:F].rearrange("(c p) n -> p c n", p=P)),
                    (K.w2_raw[0:HR, HC, :], A.ffn_w2[layer, F:HID])]

        K.local_loads, K.mlp_loads = local_loads, mlp_loads
        K.local_in, K.mlp_in = count("local_in"), count("mlp_in")
        K.rows_stored = [count(f"rows_stored{r}", 16) for r in range(2)]
        with nc.Block() as block:

            @block.gpsimd
            def _(pool):
                for c in credited:
                    pool.sem_inc(c.sem, c.credit)

        tok_phase(nc, tok_s, mem, K, A)
        attention_phase(nc, attention_s, mem, K, A)
        for layer in range(2):
            local_phase(nc, local_s[layer], mem, K, A, layer)
            mlp_phase(nc, mlp_s[layer], mem, K, A, layer, layer == 1)


def arrays(inputs):
    import numpy as np
    out = {name.replace("L0_", ""): np.ascontiguousarray(a) for name, a in inputs.items()}
    out["tok_w"] = out.pop("tok_weight")
    out["tok_ws"] = out.pop("tok_weighted_sum")
    out["ident"] = np.eye(P, dtype=np.float32)
    half = np.arange(0, DH, 2, dtype=np.float32)
    t = np.arange(N, dtype=np.float32)
    freqs = t[:, None] * (1.0 / ROPE_BASE ** (half / DH)).astype(np.float32)[None, :]
    base = (half + 0.4 * DH) / (1.4 * DH)
    scale = base[None, :].astype(np.float32) ** ((t - N // 2) / (WINDOW // 2))[:, None].astype(np.float32)
    c, sn = np.cos(freqs), np.sin(freqs)
    both = lambda a, b: np.concatenate([a, b], 1)
    cos = np.stack([both(c * scale, c * scale), both(c / scale, c / scale)], 1)
    sin = np.stack([both(-sn * scale, sn * scale), both(-sn / scale, sn / scale)], 1)
    for name, table in (("rope_cos", cos), ("rope_sin", sin)):
        out[name] = np.ascontiguousarray(table.reshape(TB, P, 2, DH).transpose(1, 0, 2, 3).astype(np.float32))
    i, j = np.arange(P)[:, None], np.arange(P)[None, :]
    out["mask_prev"] = np.where(i > j, MASKED, 0.0).astype(np.float32)
    out["mask_cur"] = np.where(i < j, MASKED, 0.0).astype(np.float32)
    first = np.arange(T // 2) % (TB // 2) == 0
    out["flags"] = np.tile(np.where(first, 0.0, 1.0).astype(np.float32), (P, 1))
    out["negs"] = np.tile(np.where(first, MASKED, 0.0).astype(np.float32), (P, 1))
    return out


def kernel(**inputs):
    import numpy as np
    import concourse.bacc as bacc
    from concourse.bass_utils import run_bass_kernel_spmd

    nc = bacc.Bacc("TRN2", target_bir_lowering=False, num_devices=1)
    feeds = arrays(inputs)
    aps = [nc.dram_tensor(name, a.shape, mybir.dt.from_np(a.dtype), kind="ExternalInput").ap()
           for name, a in feeds.items()]
    out = nc.dram_tensor("out", (B, N, D), F32, kind="ExternalOutput").ap()
    build(nc, list(feeds), aps, out)
    result = run_bass_kernel_spmd(nc, [feeds], core_ids=[0])
    return np.asarray(result.results[0]["out"])
```
